# Optimizing a Trainium2 kernel written in Bass

```python
import numpy as np
import jax
import jax.numpy as jnp

def _softmax(x, axis=-1):
    return jax.nn.softmax(x, axis=axis)

def _gelu(x):
    return jax.nn.gelu(x, approximate=True)

def _silu(x):
    return jax.nn.silu(x)

def _sigmoid(x):
    return jax.nn.sigmoid(x)

def _layernorm(x, axis=-1, eps=1e-05):
    m = jnp.mean(x, axis=axis, keepdims=True)
    v = jnp.var(x, axis=axis, keepdims=True)
    return (x - m) / jnp.sqrt(v + eps)

def _scatter_add(tgt, idx, src, axis=0):
    return tgt.at[idx].add(src)

def _segment_sum(src, seg, n):
    return jax.ops.segment_sum(src, seg, n)
kernel_name = 'mk_cond_resid_d2_seqx_r2_135c8f'

def setup_inputs(seed: int=0):
    np.random.seed(seed)
    _w = jnp.asarray

    def _rec_inputs():
        import jax
        import jax.numpy as jnp
        _rk = jax.random.key(seed)
        x = -7.109e-05 + 0.9999 * jax.random.normal(jax.random.fold_in(_rk, 1), (64, 128, 2048), jnp.float32)
        _lenS = 128 - jax.random.randint(jax.random.fold_in(_rk, 7), (64,), 0, max(1, 128 // 4) + 1, jnp.int32)
        _lenS2 = 128 - jax.random.randint(jax.random.fold_in(_rk, 8), (64,), 0, max(1, 128 // 4) + 1, jnp.int32)
        itok_B_0_15 = jax.random.randint(jax.random.fold_in(_rk, 11), (64,), 0, 16, jnp.int32)
        itok_B_78_3631 = jax.random.randint(jax.random.fold_in(_rk, 12), (64,), 78, 1816, jnp.int32)
        return (x, itok_B_0_15, itok_B_78_3631)
    x, itok_B_0_15, itok_B_78_3631 = _rec_inputs()

    def _L0_cond_setup():
        import jax, jax.numpy as jnp
        import numpy as np
        B, C, T = (64, 128, 2048)
        S, D = (16, 128)
        key = jax.random.key(seed)
        k1, k2, k3 = jax.random.split(key, 3)
        x = jax.random.normal(k1, (B, C, T), dtype=jnp.float32)
        condition = jax.random.randint(k2, (B,), 0, S, dtype=jnp.int64)
        bound = float(np.sqrt(6.0 / C))
        weights = jax.random.uniform(k3, (S, C, D), dtype=jnp.float32, minval=-bound, maxval=bound)
        return {'x': x, 'condition': condition, 'weights': weights}
    _L0_cond_all = _L0_cond_setup()
    _L0_cond_in = {k: v for k, v in _L0_cond_all.items() if k in ('weights',)}
    del _L0_cond_all

    def _L1_cond_setup():
        import math
        import jax, jax.numpy as jnp
        import numpy as np
        B, H, N, L = (16, 128, 64, 2048)
        DT_MIN, DT_MAX = (0.001, 0.1)

        def _get_kernel(log_dt, C, log_A_real, A_imag, length):
            dt = jnp.exp(log_dt)
            Cc = C[..., 0] + 1j * C[..., 1]
            A = -jnp.exp(log_A_real) + 1j * A_imag
            dtA = A * dt[:, None]
            Ct = Cc * (jnp.exp(dtA) - 1.0) / A
            P = dtA[:, :, None] * jnp.arange(length, dtype=jnp.float32)
            K = 2.0 * jnp.einsum('hn,hnl->hl', Ct, jnp.exp(P)).real
            return K
        key = jax.random.key(seed)
        ks = jax.random.split(key, 5)
        u = jax.random.normal(ks[0], (B, H, L), dtype=jnp.float32)
        log_dt = jax.random.uniform(ks[1], (H,), dtype=jnp.float32) * (math.log(DT_MAX) - math.log(DT_MIN)) + math.log(DT_MIN)
        C = jax.random.normal(ks[2], (H, N, 2), dtype=jnp.float32)
        log_A_real = jnp.log(0.5 * jnp.ones((H, N), dtype=jnp.float32))
        A_imag = math.pi * jnp.broadcast_to(jnp.arange(N, dtype=jnp.float32), (H, N))
        D = jax.random.normal(ks[3], (H,), dtype=jnp.float32)
        length = jax.random.randint(ks[4], (B,), 1, L + 1, dtype=jnp.int32)
        return {'u': u, 'log_dt': log_dt, 'C': C, 'log_A_real': log_A_real, 'A_imag': A_imag, 'D': D, 'length': length}
    _L1_cond_all = _L1_cond_setup()
    _L1_cond_in = {k: v for k, v in _L1_cond_all.items() if k in ('log_dt', 'C', 'log_A_real', 'A_imag', 'D')}
    del _L1_cond_all
    return {'x': x, 'itok_B_0_15': itok_B_0_15, 'itok_B_78_3631': itok_B_78_3631, 'L0_cond_weights': _L0_cond_in['weights'], 'L1_cond_log_dt': _L1_cond_in['log_dt'], 'L1_cond_C': _L1_cond_in['C'], 'L1_cond_log_A_real': _L1_cond_in['log_A_real'], 'L1_cond_A_imag': _L1_cond_in['A_imag'], 'L1_cond_D': _L1_cond_in['D']}

def reference(x, itok_B_0_15, itok_B_78_3631, L0_cond_weights, L1_cond_log_dt, L1_cond_C, L1_cond_log_A_real, L1_cond_A_imag, L1_cond_D):
    import jax
    import jax.numpy as jnp

    def _L0_cond_ref(x, condition, weights):
        import jax, jax.numpy as jnp
        import numpy as np
        B, C, T = (64, 128, 2048)
        S, D = (16, 128)
        W = weights[condition]
        return jnp.einsum('bct,bcd->bdt', x, W)

    def _L1_cond_ref(u, log_dt, C, log_A_real, A_imag, D, length):
        import math
        import jax, jax.numpy as jnp
        import numpy as np
        B, H, N, L = (16, 128, 64, 2048)
        DT_MIN, DT_MAX = (0.001, 0.1)

        def _get_kernel(log_dt, C, log_A_real, A_imag, length):
            dt = jnp.exp(log_dt)
            Cc = C[..., 0] + 1j * C[..., 1]
            A = -jnp.exp(log_A_real) + 1j * A_imag
            dtA = A * dt[:, None]
            Ct = Cc * (jnp.exp(dtA) - 1.0) / A
            P = dtA[:, :, None] * jnp.arange(length, dtype=jnp.float32)
            K = 2.0 * jnp.einsum('hn,hnl->hl', Ct, jnp.exp(P)).real
            return K
        Bq, Hq, Lq = u.shape
        K = _get_kernel(log_dt, C, log_A_real, A_imag, Lq)
        n = 2 * Lq
        kf = jnp.fft.rfft(K, n=n)
        uf = jnp.fft.rfft(u, n=n)
        y = jnp.fft.irfft(uf * kf[None], n=n)[..., :Lq]
        y = y + u * D[:, None]
        mask = (jnp.arange(Lq)[None, :] < length[:, None]).astype(u.dtype)
        return y * mask[:, None, :]
    x = x + _L0_cond_ref(x, itok_B_0_15, L0_cond_weights)
    x = x + _L1_cond_ref(x, L1_cond_log_dt, L1_cond_C, L1_cond_log_A_real, L1_cond_A_imag, L1_cond_D, itok_B_78_3631)
    return x

_drawn_inputs = setup_inputs


def setup_inputs(seed=0):
    import zlib

    import numpy as np

    out = dict(_drawn_inputs(seed))
    spreads = {'L1_cond_log_A_real': (-0.6931471824645996, 0.2)}
    factors = {}
    for name, (base, spread) in spreads.items():
        noise = np.random.default_rng([zlib.crc32(name.encode()), seed]).standard_normal(out[name].shape)
        drawn = base * np.exp(spread * noise) if base else spread * noise
        out[name] = jnp.asarray(drawn.astype(out[name].dtype))
    for name, factor in factors.items():
        out[name] = (out[name] * factor).astype(out[name].dtype)
    return out
```

```python
import math
from contextlib import ExitStack

import concourse.bass as bass
from concourse import mybir

F32 = mybir.dt.float32
F16 = mybir.dt.float16
I32 = mybir.dt.int32
U8 = mybir.dt.uint8
ALU = mybir.AluOpType
ACT = mybir.ActivationFunctionType

P = 128
NB, H, T = 64, 128, 2048
NC = 16
NM = 64
KB = T // P
Q = 256
NJ = T // Q
BG = 16
NG = NB // BG
ROWS = NJ * BG
RUN = 2 * ROWS
NS = 9
US = 8.0
KS = 256.0
ROUND = 1.5 * 2.0 ** 23
TWO_PI_HI = 6.28125
TWO_PI_LO = 2 * math.pi - TWO_PI_HI
LN2_HI = 0.693359375
LN2_LO = math.log(2.0) - LN2_HI
KROW = 3 * P


def ap(t, offset, dims, parts=P, first=0):
    width = 1
    for n in t.shape[1:]:
        width *= n
    return bass.AP(t, offset + first * width, [[width, parts]] + [list(d) for d in dims])


def build(nc, x, cond, length, w_in, log_dt, c_in, log_a, a_im, d_in, out):
    u_dram = nc.dram_tensor("u_scratch", [H, P, 2, NG, RUN], F16, kind="Internal")
    k_dram = nc.dram_tensor("k_scratch", [H, 2, KROW], F16, kind="Internal")

    ctx = ExitStack()
    with ctx:
        def sb(name, shape, dt, where=ctx):
            return where.enter_context(nc.sbuf_tensor(name, shape, dt))

        def sem(name):
            return ctx.enter_context(nc.semaphore(name))

        x_f = [sb(f"x_f{i}", [P, T // 2], F32) for i in range(4)]
        x_hi = [sb(f"x_hi{a}", [P, T // 2], F16) for a in range(2)]
        x_lo = [sb(f"x_lo{a}", [P, T // 2], F16) for a in range(2)]
        w_pair = sb("w_pair", [P, NC, 2, H], F16)
        cond_sb = sb("cond_sb", [1, NB], I32)
        len_i = sb("len_i", [P, NG], I32)
        len_f = sb("len_f", [P, NG], F32)
        row_i = sb("row_i", [P, 1], I32)
        d_col = sb("d_col", [P, 1], F32)
        flip = sb("flip", [P, P], F16)
        sign = sb("sign", [P, P], F16)
        diag = sb("diag", [P, P], F16)
        cross = sb("cross", [P, P], F16)
        a_re, a_imt = (sb(f"alpha_{n}", [P, H, 16], F32) for n in ("re", "im"))
        b_re, b_imt = (sb(f"beta_{n}", [P, H, 16], F32) for n in ("re", "im"))
        s_re, s_im, k_a, k_b, c_top = (sb(n, [P, H], F32) for n in ("s_re", "s_im", "k_a", "k_b", "c_top"))
        lam_rh, lam_rl, lam_ih = (sb(f"lam_{n}", [P, H], F32) for n in ("rh", "rl", "ih"))
        tmp_t = sb("tmp_t", [P, 256], F32)
        powers = ExitStack()
        pw_re, pw_im = (sb(f"pw_{n}", [P, NS, H], F32, powers) for n in ("re", "im"))
        powers.close()
        k_lhs = sb("k_lhs", [P, H, 16], F32)
        lam_il = sb("lam_il", [P, H], F32)
        sb("lam_pad", [P, H], F32)
        lam = [[lam_rh, lam_rl], [lam_ih, lam_il]]

        start = ExitStack()
        ident = sb("ident", [P, P], F32, start)
        w_f = sb("w_f", [P, NC, H], F32, start)
        w_8 = sb("w_8", [P, NC, H], F32, start)
        nat = [sb(f"nat{i}", [P, 2 * P], F32, start) for i in range(3)]
        logs = sb("logs", [P, 2, H], F32, start)
        exps = sb("exps", [P, 2, H], F32, start)
        turns = sb("turns", [P, 2 * NS + 1, H], F32, start)
        waves = sb("waves", [P, 2 * NS + 1, H], F32, start)
        big = [sb(f"big{i}", [P, NS, H], F32, start) for i in range(6)]
        big_i = sb("big_i", [P, NS, H], I32, start)
        sm = [sb(f"sm{i}", [P, H], F32, start) for i in range(24)]
        start.close()

        loop_b = ExitStack()
        u_stage = [sb(f"u_stage{i}", [P, H, RUN], F16, loop_b) for i in range(2)]
        loop_b.close()

        k_body = [sb(f"k_body_{n}", [16, H, 16], F16) for n in ("hi", "lo")]
        k_head = sb("k_head", [P, 2, P], F16)
        k_zero = sb("k_zero", [P, 4], F32)
        u_sb = [sb(f"u_sb{i}", [P, 2, 2, NG, 2, ROWS], F16) for i in range(4)]
        toep = [sb(f"toep{i}", [P, 2, 2, Q], F16) for i in range(2)]
        g_sb = [sb(f"g_sb{i}", [P, 2, 2, Q], F16) for i in range(4)]
        g_x = [sb(f"g_x{i}", [P, 2, Q], F32) for i in range(2)]
        g_y = [sb(f"g_y{i}", [P, 2, Q], F32) for i in range(2)]
        gt_sb = [sb(f"gt_sb{i}", [P, 2, 2, 2, P], F16) for i in range(2)]
        lam_sb = [sb(f"lam_sb{i}", [P, 2, 2, P], F16) for i in range(2)]
        lam_t = sb("lam_t", [P, 4, P], F16)
        st_sb = [sb(f"st_sb{i}", [P, 2, 2, NG, NJ, BG], F16) for i in range(2)]
        o_sb = [sb(f"o_sb{i}", [P, NG, Q], F32) for i in range(4)]
        mask_i = sb("mask_i", [P, Q], I32)
        mask = sb("mask", [P, NG, Q], U8)

        bank = ctx.enter_context(nc.psum_tensor("bank", [P, 8, 512], F32))

        s_in = [sem(f"s_in{i}") for i in range(5)]
        s_const = sem("s_const")
        s_tr = sem("s_tr")
        s_dve = sem("s_dve")
        s_turn = sem("s_turn")
        s_wave = sem("s_wave")
        s_coef = sem("s_coef")
        s_wp = sem("s_wp")
        s_x = [sem(f"s_x{i}") for i in range(4)]
        s_xh, s_xl, s_mm, s_uh, s_ul = (sem(n) for n in ("s_xh", "s_xl", "s_mm", "s_uh", "s_ul"))
        s_stage = [sem(f"s_stage{i}") for i in range(2)]
        s_tab = sem("s_tab")
        s_msk = sem("s_msk")
        s_km, s_kh, s_kl, s_kd = (sem(n) for n in ("s_km", "s_kh", "s_kl", "s_kd"))
        s_u = [sem(f"s_u{i}") for i in range(4)]
        s_t = [sem(f"s_t{i}") for i in range(2)]
        s_gx, s_gw, s_g, s_lt, s_lam, s_gt, s_gte = (
            sem(n) for n in ("s_gx", "s_g3", "s_g", "s_lt", "s_lam", "s_gt", "s_gte"))
        s_st, s_sth, s_stl, s_out = (sem(n) for n in ("s_st", "s_sth", "s_stl", "s_out"))
        s_o1 = [sem(f"s_o1{i}") for i in range(2)]
        s_o2 = [sem(f"s_o2{i}") for i in range(2)]
        s_store = [sem(f"s_store{i}") for i in range(4)]

        N_BANKS = 4 * NB
        block = ctx.enter_context(nc.Block())

        class Chain:
            def __init__(self, eng, s):
                self.eng, self.s, self.n = eng, s, 0

            def __call__(self, ins):
                ins.then_inc(self.s, 1)
                self.n += 1
                self.eng.wait_ge(self.s, self.n)

        def first_peeled(eng, body):
            def group(G, half, start):
                with eng.Fori(start, 4) as quarter:
                    body(G, half, quarter)
            body(0, 0, 0)
            group(0, 0, 1)
            group(0, 1, 0)
            with eng.Fori(1, NG) as G:
                group(G, 0, 0)
                group(G, 1, 0)

        def unit(G, half, quarter, r):
            return 32 * G + 16 * half + 4 * quarter + r

        PAIRS = H // 2
        PEELED = 3
        LOOPS = (PAIRS - PEELED - 2) // 4

        def slots(eng, body):
            for s in range(PEELED):
                body(0, s)
            with eng.Fori(0, LOOPS) as i:
                for c in range(PEELED, PEELED + 4):
                    body(i, c)
            for s in range(4 * LOOPS + PEELED, PAIRS + 1):
                body(0, s)

        def has(i, c):
            return not isinstance(i, int) or 0 <= c < PAIRS

        def wait(eng, s, value):
            if not isinstance(value, int) or value > 0:
                eng.wait_ge(s, value)

        def state(t, part, j):
            return ap(t, part * NG * ROWS + j * BG, [[2 * NG * ROWS, 2], [ROWS, NG], [1, BG]])

        def new_state(j):
            return bank[:, 0:2, (j - 1) * NB:j * NB].rearrange("p h (g b) -> p h g b", b=BG)

        @block.sync
        def _(sp):
            sp.dma_start(nat[0][:, 0:NM], log_a[:, :]).then_inc(s_in[0], 16)
            sp.dma_start(nat[0][:, NM:P], log_a[:, :]).then_inc(s_in[0], 16)
            sp.dma_start(nat[1][:, 0:NM], a_im[:, :]).then_inc(s_in[0], 16)
            sp.dma_start(nat[1][:, NM:P], a_im[:, :]).then_inc(s_in[0], 16)
            sp.dma_start(nat[2][:, 0:P], c_in.rearrange("h n c -> h (n c)")).then_inc(s_in[0], 16)
            sp.dma_start(nat[2][:, P:2 * P], c_in.rearrange("h n c -> h (n c)")).then_inc(s_in[0], 16)
            sp.dma_start(logs[:, 0, :], log_dt.partition_broadcast(P)).then_inc(s_in[1], 16)
            sp.dma_start(w_f[:, :, :], w_in.rearrange("s c d -> c s d")).then_inc(s_in[2], 16)
            sp.dma_start(cond_sb[:, :], cond.rearrange("(a b) -> a b", a=1)).then_inc(s_in[3], 16)
            for j in range(NJ):
                sp.dma_start(len_i[j * BG:(j + 1) * BG, :], length.rearrange("(g b) -> b g", b=BG),
                             allow_slow_non_contiguous=True)\
                    .then_inc(s_in[4], 16)
            sp.dma_start(d_col[:, :], d_in.rearrange("(h a) -> h a", a=1)).then_inc(s_in[4], 16)

            def load_x(G, half, quarter):
                for r in range(4):
                    wait(sp, s_xl, unit(G, half, quarter, r) - 3)
                    blocks = x[16 * G + 4 * quarter + r, :, :].rearrange("c (j a t) -> c j a t", a=2, t=P)
                    sp.dma_start(x_f[r][:, :].rearrange("c (j t) -> c j t", t=P), blocks[:, :, half, :])\
                        .then_inc(s_x[r], 16)

            first_peeled(sp, load_x)

            sp.wait_ge(s_stage[0], 32 * NG)
            sp.wait_ge(s_stage[1], 32 * NG)

            def load_u(i, c):
                wait(sp, s_out, 16 * i + 4 * (c - 3))
                sp.dma_start(u_sb[c % 4][:, :, :, :, :, :].rearrange("p h a g k r -> p h (a g k r)"),
                             u_dram.ap()[bass.ds(8 * i + 2 * c, 2), :, :, :, :].rearrange("h p a g r -> p h (a g r)"))\
                    .then_inc(s_u[c % 4], 16)

            def load_toeplitz(i, c):
                src = bass.AP(k_dram, (8 * i + 2 * c) * (2 * KROW), [[1, P], [KROW, 4], [1, Q]])
                sp.dma_start(toep[c % 2][:, :, :, :].rearrange("p h a t -> p (h a) t"), src)\
                    .then_inc(s_t[c % 2], 16)

            load_u(0, 0)
            load_u(0, 1)
            sp.wait_ge(s_kh, 1)
            sp.wait_ge(s_kl, 1)
            for k in range(2):
                dst = bass.AP(k_dram, k * KROW + P, [[16, 16], [2 * KROW, H], [1, 16]])
                sp.dma_start(dst, k_body[k][:, :, :]).then_inc(s_kd, 16)
            sp.dma_start(k_dram.ap()[:, :, 0:P], k_head[:, :, :]).then_inc(s_kd, 16)
            sp.wait_ge(s_kd, 48)

            def slot(i, c):
                if has(i, c):
                    wait(sp, s_out, 16 * i + 4 * (c - 1))
                    load_toeplitz(i, c)
                if has(i, c + 2):
                    load_u(i, c + 2)
                if has(i, c - 1):
                    for h in range(2):
                        o = 2 * ((c - 1) % 2) + h
                        for g in range(NG):
                            if g % 2 == 0:
                                wait(sp, s_o2[g // 2], 8 * i + 2 * (c - 1) + h + 1)
                            dst = bass.AP(out.tensor, (8 * i + 2 * (c - 1) + h) * T + g * (BG * H * T),
                                          [[Q, NJ], [H * T, BG], [1, Q]])
                            sp.dma_start(dst, o_sb[o][:, g, :]).then_inc(s_store[o], 16)

            slots(sp, slot)
            for o in range(4):
                sp.wait_ge(s_store[o], 64 * (PAIRS // 2))

        @block.gpsimd
        def _(pool):
            do = Chain(pool, s_const)
            do(pool.memset(ident[:, :], 0.0))
            do(pool.affine_select(out=ident[:, :], in_=ident[:, :], compare_op=ALU.not_equal, fill=1.0,
                                  base=0, pattern=[[-1, P]], channel_multiplier=1))
            pool.wait_ge(s_in[2], 16)
            do(pool.tensor_tensor(out=w_8[:, :, :], in0=w_f[:, :, :],
                                  in1=ap(ident, 0, [[0, NC], [1, P]]), op=ALU.add))
            do(pool.tensor_scalar(w_8[:, :, :], w_8[:, :, :], US, None, ALU.mult))
            do(pool.tensor_copy(w_pair[:, :, 0, :], w_8[:, :, :]))
            do(pool.tensor_tensor(out=w_pair[:, :, 1, :], in0=w_8[:, :, :], in1=w_pair[:, :, 0, :],
                                  op=ALU.subtract))
            pool.sem_inc(s_wp, 1)
            for m in (flip, sign, diag, cross):
                do(pool.memset(m[:, :], 0.0))
            do(pool.affine_select(out=flip[:, :], in_=flip[:, :], compare_op=ALU.not_equal, fill=1.0 / US,
                                  base=-(P - 1), pattern=[[1, P]], channel_multiplier=1))
            do(pool.affine_select(out=diag[:, :], in_=diag[:, :], compare_op=ALU.not_equal, fill=1.0,
                                  base=0, pattern=[[-1, P]], channel_multiplier=1))
            for lo, col, m, fill in ((0, 0, sign, 1.0), (NM, NM, sign, -1.0),
                                     (0, NM, cross, 1.0), (NM, 0, cross, -1.0)):
                part = m[lo:lo + NM, col:col + NM]
                do(pool.affine_select(out=part, in_=part, compare_op=ALU.not_equal, fill=fill,
                                      base=0, pattern=[[-1, NM]], channel_multiplier=1))
            pool.wait_ge(s_coef, 1)
            for lo, sg in ((0, 1.0), (NM, -1.0)):
                rows = slice(lo, lo + NM)
                for t, s in ((a_re, s_re), (a_imt, s_im)):
                    do(pool.tensor_scalar(t[rows, :, 0:1].rearrange("p h a -> p (h a)"), s[rows, :], sg, None, ALU.mult))
            do(pool.memset(b_re[0:NM, :, 0:1], 1.0))
            do(pool.memset(b_imt[0:NM, :, 0:1], 0.0))
            do(pool.memset(b_re[NM:P, :, 0:1], 0.0))
            do(pool.memset(b_imt[NM:P, :, 0:1], -1.0))

            def product(dst, p1, f1, p2, f2, op, z0, z, hn):
                for h0 in range(0, H, hn):
                    v = lambda t, o: ap(t, h0 * 16 + o, [[16, hn], [1, z]])
                    f = lambda t, o: ap(t, o + h0, [[1, hn], [0, z]])
                    tmp = ap(tmp_t, 0, [[z, hn], [1, z]])
                    do(pool.tensor_tensor(out=v(dst, z0), in0=v(p1, 0), in1=f(*f1), op=ALU.mult))
                    do(pool.tensor_tensor(out=tmp, in0=v(p2, 0), in1=f(*f2), op=ALU.mult))
                    do(pool.tensor_tensor(out=v(dst, z0), in0=v(dst, z0), in1=tmp, op=op))

            for re, im, s0 in ((b_re, b_imt, 0), (a_re, a_imt, 4)):
                for lv in range(4):
                    z, fr, fi = 1 << lv, (pw_re, (s0 + lv) * H), (pw_im, (s0 + lv) * H)
                    hn = min(H, 256 // z)
                    product(re, re, fr, im, fi, ALU.subtract, z, z, hn)
                    product(im, re, fi, im, fr, ALU.add, z, z, hn)
            for (hi, lo), t in zip(lam, (pw_re, pw_im)):
                half = tmp_t[:, 0:NM].bitcast(F16)
                do(pool.tensor_copy(half, t[:, NS - 1, :]))
                do(pool.tensor_copy(hi[:, :], half))
                do(pool.tensor_tensor(out=lo[:, :], in0=t[:, NS - 1, :], in1=hi[:, :], op=ALU.subtract))
            product(k_lhs, a_re, (k_a, 0), a_imt, (k_b, 0), ALU.add, 0, 16, 16)
            pool.sem_inc(s_tab, 1)
            pool.wait_ge(s_stage[0], 32 * NG)
            pool.wait_ge(s_stage[1], 32 * NG)
            do(pool.iota(mask_i[:, :], pattern=[[1, Q]], base=0, channel_multiplier=0))
            do(pool.iota(row_i[:, :], pattern=[[0, 1]], base=0, channel_multiplier=Q // BG))
            for t in st_sb:
                do(pool.memset(t[:, :, :, :, 0, :], 0.0))
            pool.sem_inc(s_msk, 1)

            def outer(i, c):
                r = c % 2
                wait(pool, s_g, 4 * i + c - 1)
                for dst, ta, tb in ((g_x, a_re, b_re), (g_y, a_imt, b_imt)):
                    for h in range(2):
                        o = (8 * i + 2 * c + h) * 16
                        pool.tensor_tensor(out=ap(dst[r], h * Q, [[16, 16], [1, 16]]),
                                           in0=ap(ta, o, [[1, 16], [0, 16]]),
                                           in1=ap(tb, o, [[0, 16], [1, 16]]), op=ALU.mult).then_inc(s_gx, 1)

            outer(0, 0)

            def slot(i, c):
                if has(i, c + 1):
                    outer(i, c + 1)

            slots(pool, slot)

        @block.tensor
        def _(pe):
            pe.wait_ge(s_const, 2)
            pe.wait_ge(s_in[0], 96)
            srcs = [nat[0][:, 0:P], nat[1][:, 0:P],
                    ap(nat[2], 0, [[P, 2], [2, NM]]), ap(nat[2], 1, [[P, 2], [2, NM]])]
            for k, src in enumerate(srcs):
                last = pe.transpose(bank[:, k, 0:P], src, ident[:, :])
            last.then_inc(s_tr, 1)
            pe.wait_ge(s_in[3], 16)
            pe.wait_ge(s_wp, 1)
            pe.wait_ge(s_coef, 1)

            pe.sem_inc(s_mm, 2)

            def mix(G, half, quarter):
                for r in range(4):
                    n = unit(G, half, quarter, r)
                    sel = pe.value_load(cond_sb[0:1, bass.ds(16 * G + 4 * quarter + r, 1)], min_val=0, max_val=NC - 1)
                    wait(pe, s_xh, n + 1)
                    wait(pe, s_xl, n + 1)
                    wait(pe, s_ul, 2 * n - 6)
                    for j in range(NJ):
                        back = slice((NJ - 1 - j) * P, (NJ - j) * P)
                        dst = bank[:, 2 * r + j // 4, (j % 4) * H:(j % 4 + 1) * H]
                        for m, (xs, part) in enumerate(((x_hi, 0), (x_hi, 1), (x_lo, 0))):
                            last = pe.matmul(dst, xs[r % 2][:, back],
                                             ap(w_pair, sel * (2 * H) + part * H, [[1, H]]),
                                             start=(m == 0), stop=(m == 2))
                        if j % 4 == 3:
                            last.then_inc(s_mm, 1)

            first_peeled(pe, mix)

            pe.wait_ge(s_ul, N_BANKS)
            pe.wait_ge(s_tab, 1)
            for h in range(H):
                pe.matmul(bank[0:16, h // 32, (h % 32) * 16:(h % 32 + 1) * 16], k_lhs[:, h, :],
                          b_re[:, h, :], start=True, stop=True)
            pe.matmul(bank[:, 4, 0:1], c_top[:, :], b_re[:, 0, 0:1], start=True, stop=True)\
                .then_inc(s_km, 1)

            def transpose_g(i, c):
                wait(pe, s_g, 4 * i + c + 1)
                wait(pe, s_gte, 8 * i + 2 * c)
                for h in range(2):
                    for tb in range(2):
                        for part in range(2):
                            last = pe.matmul(bank[:, 6 + h, (2 * tb + part) * P:(2 * tb + part + 1) * P],
                                             g_sb[c % 4][:, h, part, (1 - tb) * P:(2 - tb) * P], sign[:, :],
                                             start=True, stop=True)
                    last.then_inc(s_gt, 1)

            SPLIT = ((0, 0), (1, 0), (0, 1))

            def inputs_to_state(i, c):
                wait(pe, s_gte, 8 * i + 2 * c + 2)
                wait(pe, s_u[c % 4], 16 * (i + c // 4 + 1))
                wait(pe, s_stl, 28 * i + 7 * c)
                for h in range(2):
                    for m, (tb, (a, b)) in enumerate((tb, ab) for tb in range(2) for ab in SPLIT):
                        last = pe.matmul(bank[:, h, 0:(NJ - 1) * NB], gt_sb[c % 2][:, h, tb, a, :],
                                         ap(u_sb[c % 4], (2 * h + tb) * NG * RUN + b * ROWS,
                                            [[BG, NJ - 1], [RUN, NG], [1, BG]]),
                                         start=(m == 0), stop=(m == 5))
                last.then_inc(s_st, 1)

            def advance(i, c, j):
                wait(pe, s_lam, 4 * i + c + 1)
                wait(pe, s_sth, 28 * i + 7 * c + j)
                wait(pe, s_stl, 28 * i + 7 * c + j)
                for h in range(2):
                    for m, (a, b) in enumerate(SPLIT):
                        last = pe.matmul(bank[:, h, j * NB:(j + 1) * NB], lam_sb[c % 2][:, h, a, :],
                                         st_sb[c % 2][:, h, b, :, j, :], start=False, stop=(m == 2),
                                         skip_group_check=True)
                last.then_inc(s_st, 1)

            def out_part(i, c, n):
                h, gr = n // 4, n % 4
                u, g, t, st = u_sb[c % 4], g_sb[c % 4], toep[c % 2], st_sb[c % 2]
                y, ut = 2 + (n // 2) % 2, 4 + (n // 2) % 2
                col = (gr % 2) * Q
                if n == 0:
                    wait(pe, s_t[c % 2], 16 * (2 * i + c // 2 + 1))
                if n % 2 == 0:
                    wait(pe, s_o1[n // 2 % 2], 8 * i + 2 * c + n // 4)
                    wait(pe, s_o2[n // 2 % 2], 8 * i + 2 * c + n // 4)
                first = True
                for tb in range(2):
                    for a in range(2):
                        lhs = u[:, h, tb, gr, a, :]
                        for b in range(2 - a):
                            pe.matmul(bank[:, y, col + tb * P:col + Q], lhs, t[:, h, b, 0:Q - tb * P],
                                      start=first, stop=False, skip_group_check=True)
                            first = False
                        pe.matmul(bank[:, ut, col + tb * P:col + (tb + 1) * P], lhs, flip[:, :],
                                  start=(a == 0), stop=(a == 1), skip_group_check=True)
                for m, (a, b) in enumerate(SPLIT):
                    last = pe.matmul(bank[:, y, col:col + Q], st[:, h, a, gr, :, :].rearrange("p j b -> p (j b)"),
                                     g[:, h, b, :], start=False, stop=(m == 2), skip_group_check=True)
                if n % 2 == 1:
                    last.then_inc(s_out, 1)

            transpose_g(0, 0)
            pe.wait_ge(s_msk, 1)

            def slot(i, c):
                now, before, after = has(i, c), has(i, c - 1), has(i, c + 1)
                if now:
                    inputs_to_state(i, c)
                for n in range(8):
                    if n == 6 and after:
                        transpose_g(i, c + 1)
                    if before:
                        if n == 0:
                            wait(pe, s_sth, 28 * i + 7 * c)
                            wait(pe, s_stl, 28 * i + 7 * c)
                        out_part(i, c - 1, n)
                    if now and n < NJ - 2:
                        advance(i, c, n + 1)

            slots(pe, slot)

        @block.scalar
        def _(act):
            act.wait_ge(s_turn, 1)
            act.activation(waves[:, :, :], turns[:, :, :], ACT.Sin, scale=6.283185).then_inc(s_wave, 1)
            act.wait_ge(s_coef, 1)
            act.wait_ge(s_wp, 1)

            def split_x(G, half, quarter, r):
                n = unit(G, half, quarter, r)
                wait(act, s_x[r], 16 * (8 * G + 4 * half + quarter + 1))
                act.wait_ge(s_mm, 2 * n)
                act.activation(x_hi[r % 2][:, :], x_f[r][:, ::-1], ACT.Copy).then_inc(s_xh, 1)

            def evac(G, half, quarter, r):
                for k in range(2):
                    act.wait_ge(s_mm, 2 * unit(G, half, quarter, r) + k + 3)
                    act.activation(ap(u_stage[half], 4 * k * BG + 4 * quarter + r, [[BG, 4], [RUN, H]]),
                                   bank[:, 2 * r + k, :].rearrange("p (k d) -> p k d", k=4),
                                   ACT.Copy).then_inc(s_uh, 1)

            def store(G, half):
                act.wait_ge(s_ul, 2 * unit(G, half, 4, 0))
                for hh in range(2):
                    hs = slice(hh * H // 2, (hh + 1) * H // 2)
                    act.dma_start(u_dram.ap()[hs, :, half, G, :].rearrange("h p r -> p h r"),
                                  u_stage[half][:, hs, :]).then_inc(s_stage[half], 16)

            def group(G, half, before):
                wait(act, s_stage[half], 32 * G)
                for r in range(4):
                    split_x(G, half, 0, r)
                    if r:
                        evac(G, half, 0, r - 1)
                    elif before:
                        store(*before)
                with act.Fori(1, 4) as quarter:
                    for r in range(4):
                        split_x(G, half, quarter, r)
                        if r:
                            evac(G, half, quarter, r - 1)
                        else:
                            evac(G, half, quarter - 1, 3)
                evac(G, half, 3, 3)

            group(0, 0, None)
            group(0, 1, (0, 0))
            with act.Fori(1, NG) as G:
                group(G, 0, (G - 1, 1))
                group(G, 1, (G, 0))
            store(NG - 1, 1)

            act.wait_ge(s_km, 1)
            act.wait_ge(s_stage[0], 32 * NG)
            act.wait_ge(s_stage[1], 32 * NG)
            act.activation(k_body[0][:, :, :].rearrange("p h a -> p (h a)"),
                           bank[0:16, 0:4, :].rearrange("p a b -> p (a b)"), ACT.Copy).then_inc(s_kh, 1)

            def evac_gt(i, c):
                for h in range(2):
                    wait(act, s_gt, 8 * i + 2 * c + h + 1)
                    wait(act, s_st, 28 * i + 7 * (c - 1) - 6)
                    act.activation(gt_sb[c % 2][:, h, :, :, :].rearrange("p a b m -> p (a b m)"),
                                   bank[:, 6 + h, :], ACT.Copy).then_inc(s_gte, 1)

            def state_hi(i, c, j):
                wait(act, s_st, 28 * i + 7 * c + j)
                if j == 1:
                    wait(act, s_out, 16 * i + 4 * (c - 1))
                act.activation(state(st_sb[c % 2], 0, j), new_state(j), ACT.Copy).then_inc(s_sth, 1)

            def out_evac(i, c, v):
                o = 2 * (c % 2) + v // 2
                wait(act, s_out, 16 * i + 4 * c + v + 1)
                if v % 2 == 0:
                    wait(act, s_store[o], 64 * (2 * i + c // 2))
                act.activation(o_sb[o][:, 2 * (v % 2):2 * (v % 2) + 2, :].rearrange("p g t -> p (g t)"),
                               bank[:, 2 + v % 2, :], ACT.Copy, scale=1.0 / (US * KS)).then_inc(s_o1[v % 2], 1)

            evac_gt(0, 0)

            def slot(i, c):
                now, before, after = has(i, c), has(i, c - 1), has(i, c + 1)
                for what in ("s1", "s2", "o0", "s3", "s4", "o1", "s5", "s6", "o2", "g", "s7", "o3"):
                    k = int(what[1:] or 0)
                    if what[0] == "s" and now:
                        state_hi(i, c, k)
                    if what[0] == "o" and before:
                        out_evac(i, c - 1, k)
                    if what[0] == "g" and after:
                        evac_gt(i, c + 1)

            slots(act, slot)

        @block.vector
        def _(dve):
            do = Chain(dve, s_dve)

            def ts(o, a, s1, s2, op0, op1=None):
                do(dve.tensor_scalar(o, a, s1, s2, op0, op1) if op1 else dve.tensor_scalar(o, a, s1, None, op0))

            def tt(o, a, b, op):
                do(dve.tensor_tensor(out=o, in0=a, in1=b, op=op))

            def stt(o, a, s, b, op0, op1):
                do(dve.scalar_tensor_tensor(out=o, in0=a, scalar=s, in1=b, op0=op0, op1=op1))

            MUL, ADD, SUB = ALU.mult, ALU.add, ALU.subtract

            def exponential(o, v, k, r, p, ki):
                ts(r, v, 88.0, -87.0, ALU.min, ALU.max)
                ts(k, r, 1 / math.log(2.0), ROUND, MUL, ADD)
                ts(k, k, ROUND, None, SUB)
                stt(r, k, -LN2_HI, r, MUL, ADD)
                stt(r, k, -LN2_LO, r, MUL, ADD)
                ts(p, r, 1 / 5040, None, MUL)
                for d in (720, 120, 24, 6, 2, 1):
                    stt(p, p, 1 / d, r, ADD, MUL)
                ts(ki, k, 127.0, 2.0 ** 23, ADD, MUL)
                stt(o, p, 1.0, ki.bitcast(F32), ADD, MUL)

            def rsqrt(y, d, t):
                ts(y.bitcast(I32), d.bitcast(I32), -0.5, float(0x5F3759DF), MUL, ADD)
                for _ in range(3):
                    tt(t, y, y, MUL)
                    tt(t, t, d, MUL)
                    ts(t, t, -0.5, 1.5, MUL, ADD)
                    tt(y, y, t, MUL)

            dve.wait_ge(s_in[1], 16)
            dve.wait_ge(s_tr, 1)
            do(dve.tensor_copy(logs[:, 1, :], bank[:, 0, 0:P]))
            b2 = [t[:, 0:2, :] for t in big[:3]]
            exponential(exps[:, :, :], logs[:, :, :], *b2, big_i[:, 0:2, :])
            dt, e_re = exps[:, 0, :], exps[:, 1, :]
            (ai, cr, ci, wt, f, k, dec, em1, co, si, sh, nr, ni, qr, qi, tr, ti, t1, t2, t3, pr, pi, m2, yy) = \
                [t[:, :] for t in sm]
            do(dve.tensor_copy(ai, bank[:, 1, 0:P]))
            do(dve.tensor_copy(cr, bank[:, 2, 0:P]))
            do(dve.tensor_copy(ci, bank[:, 3, 0:P]))
            tt(wt, ai, dt, MUL)
            stt(dec, e_re, -1.0, dt, MUL, MUL)
            ts(k, wt, 1 / (2 * math.pi), ROUND, MUL, ADD)
            ts(k, k, ROUND, None, SUB)
            stt(wt, k, -TWO_PI_HI, wt, MUL, ADD)
            stt(wt, k, -TWO_PI_LO, wt, MUL, ADD)
            ts(f, wt, 1 / (2 * math.pi), None, MUL)
            for s in range(NS):
                ts(turns[:, s, :], f, 2.0 ** s, None, MUL)
                ts(turns[:, NS + s, :], f, 2.0 ** s, 0.25, MUL, ADD)
                ts(big[0][:, s, :], dec, 2.0 ** s, None, MUL)
            lo9, hi9 = turns[:, 0:NS, :], turns[:, NS:2 * NS, :]
            ts(big[1][:, :, :], lo9, ROUND, ROUND, ADD, SUB)
            tt(lo9, lo9, big[1][:, :, :], SUB)
            ts(hi9, lo9, 0.25, None, ADD)
            ts(big[1][:, :, :], hi9, ROUND, ROUND, ADD, SUB)
            tt(hi9, hi9, big[1][:, :, :], SUB)
            ts(turns[:, 2 * NS, :], f, 0.5, None, MUL)
            dve.sem_inc(s_turn, 1)
            amp = big[1][:, :, :]
            exponential(amp, big[0][:, :, :], big[2][:, :, :], big[3][:, :, :], big[4][:, :, :], big_i[:, :, :])
            p2k = big_i[:, 0, :].bitcast(F32)
            tt(em1, big[4][:, 0, :], p2k, MUL)
            ts(t1, p2k, -1.0, None, ADD)
            tt(em1, em1, t1, ADD)
            dve.wait_ge(s_wave, 1)
            tt(pw_re[:, :, :], amp, waves[:, NS:2 * NS, :], MUL)
            tt(pw_im[:, :, :], amp, waves[:, 0:NS, :], MUL)
            l_re, l_im = pw_re[:, 0, :], pw_im[:, 0, :]
            tt(nr, em1, waves[:, NS, :], MUL)
            tt(t1, waves[:, 2 * NS, :], waves[:, 2 * NS, :], MUL)
            stt(nr, t1, -2.0, nr, MUL, ADD)
            tt(t1, cr, nr, MUL)
            tt(t2, ci, l_im, MUL)
            tt(qr, t1, t2, SUB)
            tt(t1, cr, l_im, MUL)
            tt(t2, ci, nr, MUL)
            tt(qi, t1, t2, ADD)
            tt(t1, e_re, e_re, MUL)
            tt(t2, ai, ai, MUL)
            tt(t1, t1, t2, ADD)
            do(dve.reciprocal(t3, t1))
            tt(t1, qi, ai, MUL)
            tt(t2, qr, e_re, MUL)
            tt(t1, t1, t2, SUB)
            tt(tr, t1, t3, MUL)
            tt(t1, qi, e_re, MUL)
            tt(t2, qr, ai, MUL)
            stt(t1, t1, -1.0, t2, MUL, SUB)
            tt(ti, t1, t3, MUL)
            ts(c_top[0:NM, :], tr[0:NM, :], 2 * KS, None, MUL)
            do(dve.memset(c_top[NM:P, :], 0.0))
            tt(t1, tr, l_re, MUL)
            tt(t2, ti, l_im, MUL)
            tt(pr, t1, t2, SUB)
            ts(pr, pr, 2 * KS, None, MUL)
            tt(t1, tr, l_im, MUL)
            tt(t2, ti, l_re, MUL)
            tt(pi, t1, t2, ADD)
            ts(pi, pi, 2 * KS, None, MUL)
            tt(t1, pr, pr, MUL)
            tt(t2, pi, pi, MUL)
            tt(m2, t1, t2, ADD)
            rsqrt(yy, m2, t1)
            tt(m2, m2, yy, MUL)
            stt(t2, pr, -1.0, pr, MUL, ALU.max)
            tt(m2, m2, t2, ADD)
            ts(m2, m2, 0.5, None, MUL)
            rsqrt(yy, m2, t1)
            tt(t1, m2, yy, MUL)
            stt(t2, pi, -1.0, pi, MUL, ALU.max)
            stt(t2, t2, 0.5, yy, MUL, MUL)
            ts(t3, pr, 0.0, None, ALU.is_ge)
            tt(k, t1, t2, SUB)
            tt(k, k, t3, MUL)
            tt(s_re[:, :], t2, k, ADD)
            tt(t1, t1, k, SUB)
            ts(t3, pi, 0.0, None, ALU.is_ge)
            ts(t3, t3, 2.0, -1.0, MUL, ADD)
            tt(s_im[:, :], t1, t3, MUL)
            do(dve.tensor_copy(k_a[0:NM, :], s_re[0:NM, :]))
            do(dve.tensor_copy(k_a[NM:P, :], s_im[NM:P, :]))
            ts(k_b[0:NM, :], s_im[0:NM, :], -1.0, None, MUL)
            do(dve.tensor_copy(k_b[NM:P, :], s_re[NM:P, :]))
            dve.wait_ge(s_in[4], 16 * (NJ + 1))
            do(dve.tensor_copy(len_f[:, :], len_i[:, :]))
            ts(d_col[:, :], d_col[:, :], KS, KS, MUL, ADD)
            dve.sem_inc(s_coef, 1)

            def split_x(G, half, quarter, r):
                dve.wait_ge(s_xh, unit(G, half, quarter, r) + 1)
                dve.tensor_tensor(out=x_lo[r % 2][:, :], in0=x_f[r][:, ::-1], in1=x_hi[r % 2][:, :],
                                  op=SUB).then_inc(s_xl, 1)

            def evac(G, half, quarter, r):
                for kk in range(2):
                    dve.wait_ge(s_uh, 2 * unit(G, half, quarter, r) + kk + 1)
                    at = 4 * kk * BG + 4 * quarter + r
                    dve.tensor_tensor(out=ap(u_stage[half], at + ROWS, [[BG, 4], [RUN, H]]),
                                      in0=bank[:, 2 * r + kk, :].rearrange("p (k d) -> p k d", k=4),
                                      in1=ap(u_stage[half], at, [[BG, 4], [RUN, H]]),
                                      op=SUB).then_inc(s_ul, 1)

            def group(G, half):
                for r in range(4):
                    split_x(G, half, 0, r)
                    if r:
                        evac(G, half, 0, r - 1)
                with dve.Fori(1, 4) as quarter:
                    for r in range(4):
                        split_x(G, half, quarter, r)
                        if r:
                            evac(G, half, quarter, r - 1)
                        else:
                            evac(G, half, quarter - 1, 3)
                evac(G, half, 3, 3)

            with dve.Fori(0, NG) as G:
                group(G, 0)
                group(G, 1)

            dve.wait_ge(s_kh, 1)
            do(dve.tensor_tensor(out=k_body[1][:, :, :].rearrange("p h a -> p (h a)"),
                                 in0=bank[0:16, 0:4, :].rearrange("p a b -> p (a b)"),
                                 in1=k_body[0][:, :, :].rearrange("p h a -> p (h a)"), op=SUB))
            do(dve.memset(k_head[:, :, :], 0.0))
            tt(k_zero[:, 0:1], bank[:, 4, 0:1], d_col[:, :], ADD)
            do(dve.tensor_copy(k_head[:, 0, P - 1:P], k_zero[:, 0:1]))
            tt(k_head[:, 1, P - 1:P], k_zero[:, 0:1], k_head[:, 0, P - 1:P], SUB)
            dve.sem_inc(s_kl, 1)
            dve.wait_ge(s_msk, 1)
            ts(row_i[:, :], row_i[:, :], NJ * Q - Q, None, ALU.bitwise_and)
            do(dve.tensor_copy(k_zero[:, 1:2], row_i[:, :]))
            for g in range(NG):
                tt(len_f[:, g:g + 1], len_f[:, g:g + 1], k_zero[:, 1:2], SUB)
                ts(mask[:, g, :], mask_i[:, :], len_f[:, g:g + 1], None, ALU.is_ge)
            dve.wait_ge(s_tab, 1)

            def make_g(i, c):
                r = c % 2
                wait(dve, s_gx, 16 * i + 4 * c + 4)
                wait(dve, s_out, 16 * i + 4 * (c - 2))
                dve.tensor_tensor(out=g_x[r][:, :, :], in0=g_x[r][:, :, :], in1=g_y[r][:, :, :], op=SUB)\
                    .then_inc(s_gw, 1)
                dve.wait_ge(s_gw, 8 * i + 2 * c + 1)
                dve.tensor_copy(g_sb[c % 4][:, :, 0, :], g_x[r][:, :, :]).then_inc(s_gw, 1)
                dve.wait_ge(s_gw, 8 * i + 2 * c + 2)
                dve.tensor_tensor(out=g_sb[c % 4][:, :, 1, :], in0=g_x[r][:, :, :],
                                  in1=g_sb[c % 4][:, :, 0, :], op=SUB).then_inc(s_g, 1)

            def make_lambda(i, c):
                wait(dve, s_st, 28 * i + 7 * (c - 1))
                for h in range(2):
                    col = bass.ds(8 * i + 2 * c + h, 1)
                    for k2 in range(2):
                        ins = dve.tensor_scalar(lam_t[:, 2 * h + k2, :], cross[:, :], lam[1][k2][:, col], None, MUL)
                ins.then_inc(s_lt, 1)
                dve.wait_ge(s_lt, 4 * i + c + 1)
                for h in range(2):
                    col = bass.ds(8 * i + 2 * c + h, 1)
                    for k2 in range(2):
                        ins = dve.scalar_tensor_tensor(out=lam_sb[c % 2][:, h, k2, :], in0=diag[:, :],
                                                       scalar=lam[0][k2][:, col], in1=lam_t[:, 2 * h + k2, :],
                                                       op0=MUL, op1=ADD)
                ins.then_inc(s_lam, 1)

            def state_lo(i, c, j):
                wait(dve, s_sth, 28 * i + 7 * c + j)
                dve.tensor_tensor(out=state(st_sb[c % 2], 1, j), in0=new_state(j),
                                  in1=state(st_sb[c % 2], 0, j), op=SUB).then_inc(s_stl, 1)

            def overlay(i, c, v):
                o = 2 * (c % 2) + v // 2
                wait(dve, s_o1[v % 2], 8 * i + 2 * c + v // 2 + 1)
                dve.memset(k_zero[0:1, 2 + v % 2:3 + v % 2], 0.0)
                g2 = slice(2 * (v % 2), 2 * (v % 2) + 2)
                dve.copy_predicated(o_sb[o][:, g2, :].rearrange("p g t -> p (g t)"),
                                    mask[:, g2, :].rearrange("p g t -> p (g t)"),
                                    bank[:, 4 + v % 2, :]).then_inc(s_o2[v % 2], 1)

            make_g(0, 0)
            make_lambda(0, 0)

            def slot(i, c):
                now, before, after = has(i, c), has(i, c - 1), has(i, c + 1)
                for what in ("s1", "g", "s2", "o0", "s3", "l", "s4", "o1", "s5", "s6", "o2", "s7", "o3"):
                    k2 = int(what[1:] or 0)
                    if what[0] == "s" and now:
                        state_lo(i, c, k2)
                    if what[0] == "o" and before:
                        overlay(i, c - 1, k2)
                    if what[0] == "g" and after:
                        make_g(i, c + 1)
                    if what[0] == "l" and after:
                        make_lambda(i, c + 1)

            slots(dve, slot)


_INS = ["x", "itok_B_0_15", "itok_B_78_3631", "L0_cond_weights", "L1_cond_log_dt", "L1_cond_C",
        "L1_cond_log_A_real", "L1_cond_A_imag", "L1_cond_D"]


def kernel(**inputs):
    import numpy as _np
    import concourse.bacc as _bacc
    from concourse import mybir as _mybir
    from concourse.bass_utils import run_bass_kernel_spmd as _run

    nc = _bacc.Bacc("TRN2", target_bir_lowering=False, num_devices=1)
    arrays, args = {}, []
    for name in _INS:
        a = _np.ascontiguousarray(inputs[name])
        arrays[f"in_{name}"] = a
        args.append(nc.dram_tensor(f"in_{name}", a.shape, _mybir.dt.from_np(a.dtype), kind="ExternalInput").ap())
    shape = arrays["in_x"].shape
    args.append(nc.dram_tensor("out_0", shape, _mybir.dt.float32, kind="ExternalOutput").ap())
    build(nc, *args)
    r = _run(nc, [arrays], core_ids=[0])
    return r.results[0]["out_0"]
```

```python
import math
from contextlib import ExitStack

import concourse.bass as bass
from concourse import mybir

F32 = mybir.dt.float32
F16 = mybir.dt.float16
I32 = mybir.dt.int32
U8 = mybir.dt.uint8
ALU = mybir.AluOpType
ACT = mybir.ActivationFunctionType

P = 128
NB, H, T = 64, 128, 2048
NC = 16
NM = 64
KB = T // P
Q = 256
NJ = T // Q
BG = 16
NG = NB // BG
ROWS = NJ * BG
RUN = 2 * ROWS
PIECES = 16
HS = H // PIECES
NS = 9
US = 8.0
KS = 256.0
ROUND = 1.5 * 2.0 ** 23
TWO_PI_HI = 6.28125
TWO_PI_LO = 2 * math.pi - TWO_PI_HI
LN2_HI = 0.693359375
LN2_LO = math.log(2.0) - LN2_HI
KROW = 3 * P


def ap(t, offset, dims, parts=P, first=0):
    width = 1
    for n in t.shape[1:]:
        width *= n
    return bass.AP(t, offset + first * width, [[width, parts]] + [list(d) for d in dims])


def build(nc, x, cond, length, w_in, log_dt, c_in, log_a, a_im, d_in, out):
    u_dram = nc.dram_tensor("u_scratch", [H, P, 2, NG, RUN], F16, kind="Internal")
    k_dram = nc.dram_tensor("k_scratch", [H, 2, KROW], F16, kind="Internal")

    ctx = ExitStack()
    with ctx:
        def sb(name, shape, dt, where=ctx):
            return where.enter_context(nc.sbuf_tensor(name, shape, dt))

        def sem(name):
            return ctx.enter_context(nc.semaphore(name))

        x_f = [sb(f"x_f{i}", [P, T // 2], F32) for i in range(4)]
        x_hi = [sb(f"x_hi{a}", [P, T // 2], F16) for a in range(2)]
        x_lo = [sb(f"x_lo{a}", [P, T // 2], F16) for a in range(2)]
        w_pair = sb("w_pair", [P, NC, 2, H], F16)
        cond_sb = sb("cond_sb", [1, NB], I32)
        len_i = sb("len_i", [P, NG], I32)
        len_f = sb("len_f", [P, NG], F32)
        row_i = sb("row_i", [P, 1], I32)
        d_col = sb("d_col", [P, 1], F32)
        flip = sb("flip", [P, P], F16)
        sign = sb("sign", [P, P], F16)
        diag = sb("diag", [P, P], F16)
        cross = sb("cross", [P, P], F16)
        scratch = ExitStack()
        waves = sb("waves", [P, 2 * NS + 1, H], F32, scratch)
        wide = [sb(f"wide{i}", [P, NS, H], F32, scratch) for i in range(4)]
        ai, cr, ci, dec, e_re = (sb(n, [P, H], F32, scratch) for n in ("ai", "cr", "ci", "dec", "e_re"))
        p2 = sb("p2", [P, NS], F32, scratch)
        quarter_turn = sb("quarter_turn", [P, 1], F32, scratch)
        scratch.close()
        a_re, a_imt = (sb(f"alpha_{n}", [P, H, 16], F32) for n in ("re", "im"))
        b_re, b_imt = (sb(f"beta_{n}", [P, H, 16], F32) for n in ("re", "im"))
        s_re, s_im, k_a, k_b, c_top = (sb(n, [P, H], F32) for n in ("s_re", "s_im", "k_a", "k_b", "c_top"))
        lam_rh, lam_rl, lam_ih = (sb(f"lam_{n}", [P, H], F32) for n in ("rh", "rl", "ih"))
        tmp_t = sb("tmp_t", [P, 256], F32)
        powers = ExitStack()
        pw_re, pw_im = (sb(f"pw_{n}", [P, NS, H], F32, powers) for n in ("re", "im"))
        powers.close()
        k_lhs = sb("k_lhs", [P, H, 16], F32)
        lam_il = sb("lam_il", [P, H], F32)
        sb("lam_pad", [P, H], F32)
        lam = [[lam_rh, lam_rl], [lam_ih, lam_il]]

        start = ExitStack()
        ident = sb("ident", [P, P], F32, start)
        w_f = sb("w_f", [P, NC, H], F32, start)
        w_8 = sb("w_8", [P, NC, H], F32, start)
        nat = [sb(f"nat{i}", [P, 2 * P], F32, start) for i in range(3)]
        logs = sb("logs", [P, 2, H], F32, start)
        exps = sb("exps", [P, 2, H], F32, start)
        turns = sb("turns", [P, NS, H], F32, start)
        turns_r = sb("turns_r", [P, NS, H], F32, start)
        turns_a = sb("turns_a", [P, NS, H], F32, start)
        ex = [sb(f"ex{i}", [P, 2, H], F32, start) for i in range(3)]
        ex_i = sb("ex_i", [P, 2, H], I32, start)
        omega, cycles, freq = (sb(n, [P, H], F32, start) for n in ("omega", "cycles", "freq"))
        start.close()

        loop_b = ExitStack()
        u_stage = [sb(f"u_stage{i}", [P, H, RUN], F16, loop_b) for i in range(2)]
        loop_b.close()

        k_body = [sb(f"k_body_{n}", [16, H, 16], F16) for n in ("hi", "lo")]
        k_head = sb("k_head", [P, 2, P], F16)
        k_zero = sb("k_zero", [P, 4], F32)
        u_sb = [sb(f"u_sb{i}", [P, 2, 2, NG, 2, ROWS], F16) for i in range(4)]
        toep = [sb(f"toep{i}", [P, 2, 2, Q], F16) for i in range(2)]
        g_sb = [sb(f"g_sb{i}", [P, 2, 2, Q], F16) for i in range(4)]
        g_x = [sb(f"g_x{i}", [P, 2, Q], F32) for i in range(2)]
        g_y = [sb(f"g_y{i}", [P, 2, Q], F32) for i in range(2)]
        gt_sb = [sb(f"gt_sb{i}", [P, 2, 2, 2, P], F16) for i in range(2)]
        lam_sb = [sb(f"lam_sb{i}", [P, 2, 2, P], F16) for i in range(2)]
        lam_t = sb("lam_t", [P, 4, P], F16)
        st_sb = [sb(f"st_sb{i}", [P, 2, 2, NG, NJ, BG], F16) for i in range(2)]
        o_sb = [sb(f"o_sb{i}", [P, NG, Q], F32) for i in range(4)]
        mask_i = sb("mask_i", [P, Q], I32)
        mask = sb("mask", [P, NG, Q], U8)

        bank = ctx.enter_context(nc.psum_tensor("bank", [P, 8, 512], F32))

        s_in = [sem(f"s_in{i}") for i in range(5)]
        s_const = sem("s_const")
        s_tr = sem("s_tr")
        s_dve = sem("s_dve")
        s_turn = sem("s_turn")
        s_wave = sem("s_wave")
        s_abs = sem("s_abs")
        s_p2 = sem("s_p2")
        s_wp = sem("s_wp")
        s_x = [sem(f"s_x{i}") for i in range(4)]
        s_xh, s_xl, s_mm, s_uh, s_ul = (sem(n) for n in ("s_xh", "s_xl", "s_mm", "s_uh", "s_ul"))
        s_stage = [sem(f"s_stage{i}") for i in range(2)]
        s_tab = sem("s_tab")
        s_msk = sem("s_msk")
        s_km, s_kh, s_kl, s_kd = (sem(n) for n in ("s_km", "s_kh", "s_kl", "s_kd"))
        s_u = [sem(f"s_u{i}") for i in range(4)]
        s_t = [sem(f"s_t{i}") for i in range(2)]
        s_gx, s_gw, s_g, s_lt, s_lam, s_gt, s_gte = (
            sem(n) for n in ("s_gx", "s_g3", "s_g", "s_lt", "s_lam", "s_gt", "s_gte"))
        s_st, s_sth, s_stl, s_out = (sem(n) for n in ("s_st", "s_sth", "s_stl", "s_out"))
        s_o1 = [sem(f"s_o1{i}") for i in range(2)]
        s_o2 = [sem(f"s_o2{i}") for i in range(2)]
        s_store = [sem(f"s_store{i}") for i in range(4)]

        N_BANKS = 4 * NB
        STORED = (16 * PIECES * NG, 16 * (PIECES * (NG - 1) + 4))
        block = ctx.enter_context(nc.Block())

        class Chain:
            def __init__(self, eng, s):
                self.eng, self.s, self.n = eng, s, 0

            def __call__(self, ins):
                ins.then_inc(self.s, 1)
                self.n += 1
                self.eng.wait_ge(self.s, self.n)

        def first_peeled(eng, body):
            def group(G, half, start):
                with eng.Fori(start, 4) as quarter:
                    body(G, half, quarter)
            body(0, 0, 0)
            group(0, 0, 1)
            group(0, 1, 0)
            with eng.Fori(1, NG) as G:
                group(G, 0, 0)
                group(G, 1, 0)

        def unit(G, half, quarter, r):
            return 32 * G + 16 * half + 4 * quarter + r

        PAIRS = H // 2
        PEELED = 3
        LOOPS = (PAIRS - PEELED - 2) // 4

        def slots(eng, body):
            for s in range(PEELED):
                body(0, s)
            with eng.Fori(0, LOOPS) as i:
                for c in range(PEELED, PEELED + 4):
                    body(i, c)
            for s in range(4 * LOOPS + PEELED, PAIRS + 1):
                body(0, s)

        def has(i, c):
            return not isinstance(i, int) or 0 <= c < PAIRS

        def wait(eng, s, value):
            if not isinstance(value, int) or value > 0:
                eng.wait_ge(s, value)

        def state(t, part, j):
            return ap(t, part * NG * ROWS + j * BG, [[2 * NG * ROWS, 2], [ROWS, NG], [1, BG]])

        def new_state(j):
            return bank[:, 0:2, (j - 1) * NB:j * NB].rearrange("p h (g b) -> p h g b", b=BG)

        @block.sync
        def _(sp):
            sp.dma_start(nat[0][:, 0:NM], log_a[:, :]).then_inc(s_in[0], 16)
            sp.dma_start(nat[0][:, NM:P], log_a[:, :]).then_inc(s_in[0], 16)
            sp.dma_start(nat[1][:, 0:NM], a_im[:, :]).then_inc(s_in[0], 16)
            sp.dma_start(nat[1][:, NM:P], a_im[:, :]).then_inc(s_in[0], 16)
            sp.dma_start(nat[2][:, 0:P], c_in.rearrange("h n c -> h (n c)")).then_inc(s_in[0], 16)
            sp.dma_start(nat[2][:, P:2 * P], c_in.rearrange("h n c -> h (n c)")).then_inc(s_in[0], 16)
            sp.dma_start(logs[:, 0, :], log_dt.partition_broadcast(P)).then_inc(s_in[1], 16)
            sp.dma_start(w_f[:, :, :], w_in.rearrange("s c d -> c s d")).then_inc(s_in[2], 16)
            sp.dma_start(cond_sb[:, :], cond.rearrange("(a b) -> a b", a=1)).then_inc(s_in[3], 16)
            for j in range(NJ):
                sp.dma_start(len_i[j * BG:(j + 1) * BG, :], length.rearrange("(g b) -> b g", b=BG),
                             allow_slow_non_contiguous=True)\
                    .then_inc(s_in[4], 16)
            sp.dma_start(d_col[:, :], d_in.rearrange("(h a) -> h a", a=1)).then_inc(s_in[4], 16)

            def load_x(G, half, quarter):
                for r in range(4):
                    wait(sp, s_xl, unit(G, half, quarter, r) - 3)
                    blocks = x[16 * G + 4 * quarter + r, :, :].rearrange("c (j a t) -> c j a t", a=2, t=P)
                    sp.dma_start(x_f[r][:, :].rearrange("c (j t) -> c j t", t=P), blocks[:, :, half, :])\
                        .then_inc(s_x[r], 16)

            first_peeled(sp, load_x)

            sp.wait_ge(s_stage[0], STORED[0])
            sp.wait_ge(s_stage[1], STORED[1])

            def load_u(i, c):
                wait(sp, s_out, 16 * i + 4 * (c - 3))
                sp.dma_start(u_sb[c % 4][:, :, :, :, :, :].rearrange("p h a g k r -> p h (a g k r)"),
                             u_dram.ap()[bass.ds(8 * i + 2 * c, 2), :, :, :, :].rearrange("h p a g r -> p h (a g r)"))\
                    .then_inc(s_u[c % 4], 16)

            def load_toeplitz(i, c):
                src = bass.AP(k_dram, (8 * i + 2 * c) * (2 * KROW), [[1, P], [KROW, 4], [1, Q]])
                sp.dma_start(toep[c % 2][:, :, :, :].rearrange("p h a t -> p (h a) t"), src)\
                    .then_inc(s_t[c % 2], 16)

            load_u(0, 0)
            load_u(0, 1)
            sp.wait_ge(s_kh, 1)
            sp.wait_ge(s_kl, 1)
            for k in range(2):
                dst = bass.AP(k_dram, k * KROW + P, [[16, 16], [2 * KROW, H], [1, 16]])
                sp.dma_start(dst, k_body[k][:, :, :]).then_inc(s_kd, 16)
            sp.dma_start(k_dram.ap()[:, :, 0:P], k_head[:, :, :]).then_inc(s_kd, 16)
            sp.wait_ge(s_kd, 48)

            def slot(i, c):
                if has(i, c):
                    wait(sp, s_out, 16 * i + 4 * (c - 1))
                    load_toeplitz(i, c)
                if has(i, c + 2):
                    load_u(i, c + 2)
                if has(i, c - 1):
                    for h in range(2):
                        o = 2 * ((c - 1) % 2) + h
                        for g in range(NG):
                            if g % 2 == 0:
                                wait(sp, s_o2[g // 2], 8 * i + 2 * (c - 1) + h + 1)
                            dst = bass.AP(out.tensor, (8 * i + 2 * (c - 1) + h) * T + g * (BG * H * T),
                                          [[Q, NJ], [H * T, BG], [1, Q]])
                            sp.dma_start(dst, o_sb[o][:, g, :]).then_inc(s_store[o], 16)

            slots(sp, slot)
            for o in range(4):
                sp.wait_ge(s_store[o], 64 * (PAIRS // 2))

        @block.gpsimd
        def _(pool):
            do = Chain(pool, s_const)
            do(pool.memset(ident[:, :], 0.0))
            do(pool.affine_select(out=ident[:, :], in_=ident[:, :], compare_op=ALU.not_equal, fill=1.0,
                                  base=0, pattern=[[-1, P]], channel_multiplier=1))
            for n in range(NS):
                do(pool.memset(p2[:, n:n + 1], 2.0 ** n))
            do(pool.memset(quarter_turn[:, :], math.pi / 2))
            pool.sem_inc(s_p2, 1)
            pool.wait_ge(s_in[2], 16)
            do(pool.tensor_tensor(out=w_8[:, :, :], in0=w_f[:, :, :],
                                  in1=ap(ident, 0, [[0, NC], [1, P]]), op=ALU.add))
            do(pool.tensor_scalar(w_8[:, :, :], w_8[:, :, :], US, None, ALU.mult))
            do(pool.tensor_copy(w_pair[:, :, 0, :], w_8[:, :, :]))
            do(pool.tensor_tensor(out=w_pair[:, :, 1, :], in0=w_8[:, :, :], in1=w_pair[:, :, 0, :],
                                  op=ALU.subtract))
            pool.sem_inc(s_wp, 1)
            for m in (flip, sign, diag, cross):
                do(pool.memset(m[:, :], 0.0))
            do(pool.affine_select(out=flip[:, :], in_=flip[:, :], compare_op=ALU.not_equal, fill=1.0 / US,
                                  base=-(P - 1), pattern=[[1, P]], channel_multiplier=1))
            do(pool.affine_select(out=diag[:, :], in_=diag[:, :], compare_op=ALU.not_equal, fill=1.0,
                                  base=0, pattern=[[-1, P]], channel_multiplier=1))
            for lo, col, m, fill in ((0, 0, sign, 1.0), (NM, NM, sign, -1.0),
                                     (0, NM, cross, 1.0), (NM, 0, cross, -1.0)):
                part = m[lo:lo + NM, col:col + NM]
                do(pool.affine_select(out=part, in_=part, compare_op=ALU.not_equal, fill=fill,
                                      base=0, pattern=[[-1, NM]], channel_multiplier=1))
            MUL, ADD, SUB = ALU.mult, ALU.add, ALU.subtract

            def ts(o, a, s1, s2, op0, op1=None):
                do(pool.tensor_scalar(o, a, s1, s2, op0, op1) if op1 else pool.tensor_scalar(o, a, s1, None, op0))

            def tt(o, a, b, op):
                do(pool.tensor_tensor(out=o, in0=a, in1=b, op=op))

            def rsqrt(y, d, t):
                ts(y.bitcast(I32), d.bitcast(I32), -0.5, float(0x5F3759DF), MUL, ADD)
                for _ in range(3):
                    tt(t, y, y, MUL)
                    tt(t, t, d, MUL)
                    ts(t, t, -0.5, 1.5, MUL, ADD)
                    tt(y, y, t, MUL)

            r, k, p, ki = (w[:, :, :] for w in wide)
            tw, amp = pw_im[:, :, :], pw_re[:, :, :]
            pool.wait_ge(s_turn, 1)
            tt(r, ap(dec, 0, [[0, NS], [1, H]]), ap(p2, 0, [[1, NS], [0, H]]), MUL)
            ts(r, r, 88.0, -87.0, ALU.min, ALU.max)
            ts(k, r, 1 / math.log(2.0), ROUND, MUL, ADD)
            ts(k, k, ROUND, None, SUB)
            for part in (LN2_HI, LN2_LO):
                ts(tw, k, -part, None, MUL)
                tt(r, r, tw, ADD)
            ts(p, r, 1 / 5040, None, MUL)
            for d in (720, 120, 24, 6, 2, 1):
                ts(p, p, 1 / d, None, ADD)
                tt(p, p, r, MUL)
            ts(ki.bitcast(I32), k, 127.0, 2.0 ** 23, ADD, MUL)
            ts(amp, p, 1.0, None, ADD)
            tt(amp, amp, ki, MUL)
            pool.wait_ge(s_wave, 1)
            tt(pw_im[:, :, :], amp, waves[:, 0:NS, :], MUL)
            tt(pw_re[:, :, :], amp, waves[:, NS:2 * NS, :], MUL)
            e2k, em1 = ki[:, 0, :], p[:, 0, :]
            tt(em1, em1, e2k, MUL)
            ts(e2k, e2k, -1.0, None, ADD)
            tt(em1, em1, e2k, ADD)
            l_re, l_im = pw_re[:, 0, :], pw_im[:, 0, :]
            (nr, qr, qi, tr, ti, t1, t2, t3, pr) = (wide[0][:, n, :] for n in range(NS))
            (pi, m2, yy, kk) = (wide[1][:, n, :] for n in range(4))
            cr_, ci_, ai_, er_ = cr[:, :], ci[:, :], ai[:, :], e_re[:, :]
            tt(nr, em1, waves[:, NS, :], MUL)
            tt(t1, waves[:, 2 * NS, :], waves[:, 2 * NS, :], MUL)
            ts(t1, t1, -2.0, None, MUL)
            tt(nr, nr, t1, ADD)

            def complex_mul(o_re, o_im, x_re, x_im, y_re, y_im):
                tt(t1, x_re, y_re, MUL)
                tt(t2, x_im, y_im, MUL)
                tt(o_re, t1, t2, SUB)
                tt(t1, x_re, y_im, MUL)
                tt(t2, x_im, y_re, MUL)
                tt(o_im, t1, t2, ADD)

            complex_mul(qr, qi, cr_, ci_, nr, l_im)
            tt(t1, er_, er_, MUL)
            tt(t2, ai_, ai_, MUL)
            tt(t1, t1, t2, ADD)
            ts(t3.bitcast(I32), t1.bitcast(I32), -1.0, float(0x7EF311C7), MUL, ADD)
            for _ in range(4):
                tt(t2, t1, t3, MUL)
                ts(t2, t2, -1.0, 2.0, MUL, ADD)
                tt(t3, t3, t2, MUL)
            ts(m2, er_, -1.0, None, MUL)
            ts(kk, ai_, -1.0, None, MUL)
            complex_mul(tr, ti, qr, qi, m2, kk)
            tt(tr, tr, t3, MUL)
            tt(ti, ti, t3, MUL)
            ts(tr, tr, 2 * KS, None, MUL)
            ts(ti, ti, 2 * KS, None, MUL)
            do(pool.tensor_copy(c_top[0:NM, :], tr[0:NM, :]))
            do(pool.memset(c_top[NM:P, :], 0.0))
            complex_mul(pr, pi, tr, ti, l_re, l_im)
            tt(t1, pr, pr, MUL)
            tt(t2, pi, pi, MUL)
            tt(m2, t1, t2, ADD)
            rsqrt(yy, m2, t1)
            tt(m2, m2, yy, MUL)
            ts(t3, pr, 0.0, None, ALU.is_ge)
            ts(t2, t3, 2.0, -1.0, MUL, ADD)
            tt(t2, t2, pr, MUL)
            tt(m2, m2, t2, ADD)
            ts(m2, m2, 0.5, None, MUL)
            rsqrt(yy, m2, t1)
            tt(t1, m2, yy, MUL)
            ts(qr, pi, 0.0, None, ALU.is_ge)
            ts(qr, qr, 2.0, -1.0, MUL, ADD)
            tt(t2, qr, pi, MUL)
            ts(t2, t2, 0.5, None, MUL)
            tt(t2, t2, yy, MUL)
            tt(kk, t1, t2, SUB)
            tt(kk, kk, t3, MUL)
            tt(s_re[:, :], t2, kk, ADD)
            tt(t1, t1, kk, SUB)
            tt(s_im[:, :], t1, qr, MUL)
            do(pool.tensor_copy(k_a[0:NM, :], s_re[0:NM, :]))
            do(pool.tensor_copy(k_a[NM:P, :], s_im[NM:P, :]))
            ts(k_b[0:NM, :], s_im[0:NM, :], -1.0, None, MUL)
            do(pool.tensor_copy(k_b[NM:P, :], s_re[NM:P, :]))
            for lo, sg in ((0, 1.0), (NM, -1.0)):
                rows = slice(lo, lo + NM)
                for t, s in ((a_re, s_re), (a_imt, s_im)):
                    do(pool.tensor_scalar(t[rows, :, 0:1].rearrange("p h a -> p (h a)"), s[rows, :], sg, None, ALU.mult))
            do(pool.memset(b_re[0:NM, :, 0:1], 1.0))
            do(pool.memset(b_imt[0:NM, :, 0:1], 0.0))
            do(pool.memset(b_re[NM:P, :, 0:1], 0.0))
            do(pool.memset(b_imt[NM:P, :, 0:1], -1.0))

            def product(dst, p1, f1, p2, f2, op, z0, z, hn):
                for h0 in range(0, H, hn):
                    v = lambda t, o: ap(t, h0 * 16 + o, [[16, hn], [1, z]])
                    f = lambda t, o: ap(t, o + h0, [[1, hn], [0, z]])
                    tmp = ap(tmp_t, 0, [[z, hn], [1, z]])
                    do(pool.tensor_tensor(out=v(dst, z0), in0=v(p1, 0), in1=f(*f1), op=ALU.mult))
                    do(pool.tensor_tensor(out=tmp, in0=v(p2, 0), in1=f(*f2), op=ALU.mult))
                    do(pool.tensor_tensor(out=v(dst, z0), in0=v(dst, z0), in1=tmp, op=op))

            for re, im, s0 in ((b_re, b_imt, 0), (a_re, a_imt, 4)):
                for lv in range(4):
                    z, fr, fi = 1 << lv, (pw_re, (s0 + lv) * H), (pw_im, (s0 + lv) * H)
                    hn = min(H, 256 // z)
                    product(re, re, fr, im, fi, ALU.subtract, z, z, hn)
                    product(im, re, fi, im, fr, ALU.add, z, z, hn)
            for (hi, lo), t in zip(lam, (pw_re, pw_im)):
                half = tmp_t[:, 0:NM].bitcast(F16)
                do(pool.tensor_copy(half, t[:, NS - 1, :]))
                do(pool.tensor_copy(hi[:, :], half))
                do(pool.tensor_tensor(out=lo[:, :], in0=t[:, NS - 1, :], in1=hi[:, :], op=ALU.subtract))
            product(k_lhs, a_re, (k_a, 0), a_imt, (k_b, 0), ALU.add, 0, 16, 16)
            pool.sem_inc(s_tab, 1)
            pool.wait_ge(s_stage[0], STORED[0])
            pool.wait_ge(s_stage[1], STORED[1])
            do(pool.iota(mask_i[:, :], pattern=[[1, Q]], base=0, channel_multiplier=0))
            do(pool.iota(row_i[:, :], pattern=[[0, 1]], base=0, channel_multiplier=Q // BG))
            for t in st_sb:
                do(pool.memset(t[:, :, :, :, 0, :], 0.0))
            pool.sem_inc(s_msk, 1)

            def outer(i, c):
                r = c % 2
                wait(pool, s_g, 4 * i + c - 1)
                for dst, ta, tb in ((g_x, a_re, b_re), (g_y, a_imt, b_imt)):
                    for h in range(2):
                        o = (8 * i + 2 * c + h) * 16
                        pool.tensor_tensor(out=ap(dst[r], h * Q, [[16, 16], [1, 16]]),
                                           in0=ap(ta, o, [[1, 16], [0, 16]]),
                                           in1=ap(tb, o, [[0, 16], [1, 16]]), op=ALU.mult).then_inc(s_gx, 1)

            outer(0, 0)

            def slot(i, c):
                if has(i, c + 1):
                    outer(i, c + 1)

            slots(pool, slot)

        @block.tensor
        def _(pe):
            pe.wait_ge(s_const, 2)
            pe.wait_ge(s_in[0], 96)
            srcs = [nat[0][:, 0:P], nat[1][:, 0:P],
                    ap(nat[2], 0, [[P, 2], [2, NM]]), ap(nat[2], 1, [[P, 2], [2, NM]])]
            for k, src in enumerate(srcs):
                last = pe.transpose(bank[:, k, 0:P], src, ident[:, :])
            last.then_inc(s_tr, 1)
            pe.wait_ge(s_in[3], 16)
            pe.wait_ge(s_wp, 1)
            pe.wait_ge(s_turn, 1)

            pe.sem_inc(s_mm, 2)

            def mix(G, half, quarter):
                for r in range(4):
                    n = unit(G, half, quarter, r)
                    sel = pe.value_load(cond_sb[0:1, bass.ds(16 * G + 4 * quarter + r, 1)], min_val=0, max_val=NC - 1)
                    wait(pe, s_xh, n + 1)
                    wait(pe, s_xl, n + 1)
                    wait(pe, s_ul, 2 * n - 6)
                    for j in range(NJ):
                        back = slice((NJ - 1 - j) * P, (NJ - j) * P)
                        dst = bank[:, 2 * r + j // 4, (j % 4) * H:(j % 4 + 1) * H]
                        for m, (xs, part) in enumerate(((x_hi, 0), (x_hi, 1), (x_lo, 0))):
                            last = pe.matmul(dst, xs[r % 2][:, back],
                                             ap(w_pair, sel * (2 * H) + part * H, [[1, H]]),
                                             start=(m == 0), stop=(m == 2))
                        if j % 4 == 3:
                            last.then_inc(s_mm, 1)

            first_peeled(pe, mix)

            pe.wait_ge(s_ul, N_BANKS)
            pe.wait_ge(s_tab, 1)
            for h in range(H):
                pe.matmul(bank[0:16, h // 32, (h % 32) * 16:(h % 32 + 1) * 16], k_lhs[:, h, :],
                          b_re[:, h, :], start=True, stop=True)
            pe.matmul(bank[:, 4, 0:1], c_top[:, :], b_re[:, 0, 0:1], start=True, stop=True)\
                .then_inc(s_km, 1)

            def transpose_g(i, c):
                wait(pe, s_g, 4 * i + c + 1)
                wait(pe, s_gte, 8 * i + 2 * c)
                for h in range(2):
                    for tb in range(2):
                        for part in range(2):
                            last = pe.matmul(bank[:, 6 + h, (2 * tb + part) * P:(2 * tb + part + 1) * P],
                                             g_sb[c % 4][:, h, part, (1 - tb) * P:(2 - tb) * P], sign[:, :],
                                             start=True, stop=True)
                    last.then_inc(s_gt, 1)

            SPLIT = ((0, 0), (1, 0), (0, 1))

            def inputs_to_state(i, c):
                wait(pe, s_gte, 8 * i + 2 * c + 2)
                wait(pe, s_u[c % 4], 16 * (i + c // 4 + 1))
                wait(pe, s_stl, 28 * i + 7 * c)
                for h in range(2):
                    for m, (tb, (a, b)) in enumerate((tb, ab) for tb in range(2) for ab in SPLIT):
                        last = pe.matmul(bank[:, h, 0:(NJ - 1) * NB], gt_sb[c % 2][:, h, tb, a, :],
                                         ap(u_sb[c % 4], (2 * h + tb) * NG * RUN + b * ROWS,
                                            [[BG, NJ - 1], [RUN, NG], [1, BG]]),
                                         start=(m == 0), stop=(m == 5))
                last.then_inc(s_st, 1)

            def advance(i, c, j):
                wait(pe, s_lam, 4 * i + c + 1)
                wait(pe, s_sth, 28 * i + 7 * c + j)
                wait(pe, s_stl, 28 * i + 7 * c + j)
                for h in range(2):
                    for m, (a, b) in enumerate(SPLIT):
                        last = pe.matmul(bank[:, h, j * NB:(j + 1) * NB], lam_sb[c % 2][:, h, a, :],
                                         st_sb[c % 2][:, h, b, :, j, :], start=False, stop=(m == 2),
                                         skip_group_check=True)
                last.then_inc(s_st, 1)

            def out_part(i, c, n):
                h, gr = n // 4, n % 4
                u, g, t, st = u_sb[c % 4], g_sb[c % 4], toep[c % 2], st_sb[c % 2]
                y, ut = 2 + (n // 2) % 2, 4 + (n // 2) % 2
                col = (gr % 2) * Q
                if n == 0:
                    wait(pe, s_t[c % 2], 16 * (2 * i + c // 2 + 1))
                if n % 2 == 0:
                    wait(pe, s_o1[n // 2 % 2], 8 * i + 2 * c + n // 4)
                    wait(pe, s_o2[n // 2 % 2], 8 * i + 2 * c + n // 4)
                first = True
                for tb in range(2):
                    for a in range(2):
                        lhs = u[:, h, tb, gr, a, :]
                        for b in range(2 - a):
                            pe.matmul(bank[:, y, col + tb * P:col + Q], lhs, t[:, h, b, 0:Q - tb * P],
                                      start=first, stop=False, skip_group_check=True)
                            first = False
                        pe.matmul(bank[:, ut, col + tb * P:col + (tb + 1) * P], lhs, flip[:, :],
                                  start=(a == 0), stop=(a == 1), skip_group_check=True)
                for m, (a, b) in enumerate(SPLIT):
                    last = pe.matmul(bank[:, y, col:col + Q], st[:, h, a, gr, :, :].rearrange("p j b -> p (j b)"),
                                     g[:, h, b, :], start=False, stop=(m == 2), skip_group_check=True)
                if n % 2 == 1:
                    last.then_inc(s_out, 1)

            transpose_g(0, 0)
            pe.wait_ge(s_msk, 1)

            def slot(i, c):
                now, before, after = has(i, c), has(i, c - 1), has(i, c + 1)
                if now:
                    inputs_to_state(i, c)
                for n in range(8):
                    if n == 6 and after:
                        transpose_g(i, c + 1)
                    if before:
                        if n == 0:
                            wait(pe, s_sth, 28 * i + 7 * c)
                            wait(pe, s_stl, 28 * i + 7 * c)
                        out_part(i, c - 1, n)
                    if now and n < NJ - 2:
                        advance(i, c, n + 1)

            slots(pe, slot)

        @block.scalar
        def _(act):
            act.wait_ge(s_turn, 1)
            act.wait_ge(s_p2, 1)
            act.activation(turns_a[:, :, :], turns[:, :, :], ACT.Abs).then_inc(s_abs, 1)
            act.activation(waves[:, 0:NS, :], turns[:, :, :], ACT.Sin, scale=6.283185)
            act.activation(waves[:, 2 * NS, :], turns[:, 0, :], ACT.Sin, scale=3.1415925)
            act.wait_ge(s_abs, 1)
            act.activation(waves[:, NS:2 * NS, :], turns_a[:, :, :], ACT.Sin, scale=-6.283185,
                           bias=quarter_turn[:, 0:1]).then_inc(s_wave, 1)
            act.wait_ge(s_wp, 1)
            act.wait_ge(s_wave, 1)

            def split_x(G, half, quarter, r):
                n = unit(G, half, quarter, r)
                wait(act, s_x[r], 16 * (8 * G + 4 * half + quarter + 1))
                act.wait_ge(s_mm, 2 * n)
                act.activation(x_hi[r % 2][:, :], x_f[r][:, ::-1], ACT.Copy).then_inc(s_xh, 1)

            def evac(G, half, quarter, r):
                for k in range(2):
                    act.wait_ge(s_mm, 2 * unit(G, half, quarter, r) + k + 3)
                    act.activation(ap(u_stage[half], 4 * k * BG + 4 * quarter + r, [[BG, 4], [RUN, H]]),
                                   bank[:, 2 * r + k, :].rearrange("p (k d) -> p k d", k=4),
                                   ACT.Copy).then_inc(s_uh, 1)

            def store(G, half, first, count=HS):
                hs = bass.ds(first, count)
                act.dma_start(u_dram.ap()[hs, :, half, G, :].rearrange("h p r -> p h r"),
                              u_stage[half][:, hs, :]).then_inc(s_stage[half], 16)

            def group(G, half, before):
                if before:
                    before_done = 2 * unit(*before, 4, 0)
                for r in range(4):
                    split_x(G, half, 0, r)
                    if r:
                        evac(G, half, 0, r - 1)
                    else:
                        wait(act, s_stage[half], 16 * PIECES * G)
                    if before:
                        wait(act, s_ul, before_done)
                        store(*before, HS * r)
                with act.Fori(1, 4) as quarter:
                    for r in range(4):
                        split_x(G, half, quarter, r)
                        if r:
                            evac(G, half, quarter, r - 1)
                        else:
                            evac(G, half, quarter - 1, 3)
                        if before:
                            store(*before, 4 * HS * quarter + HS * r)
                evac(G, half, 3, 3)

            group(0, 0, None)
            group(0, 1, (0, 0))
            with act.Fori(1, NG) as G:
                group(G, 0, (G - 1, 1))
                group(G, 1, (G, 0))
            act.wait_ge(s_ul, N_BANKS)
            for piece in range(4):
                store(NG - 1, 1, piece * (H // 4), H // 4)

            act.wait_ge(s_km, 1)
            act.wait_ge(s_stage[0], STORED[0])
            act.wait_ge(s_stage[1], STORED[1])
            act.activation(k_body[0][:, :, :].rearrange("p h a -> p (h a)"),
                           bank[0:16, 0:4, :].rearrange("p a b -> p (a b)"), ACT.Copy).then_inc(s_kh, 1)

            def evac_gt(i, c):
                for h in range(2):
                    wait(act, s_gt, 8 * i + 2 * c + h + 1)
                    wait(act, s_st, 28 * i + 7 * (c - 1) - 6)
                    act.activation(gt_sb[c % 2][:, h, :, :, :].rearrange("p a b m -> p (a b m)"),
                                   bank[:, 6 + h, :], ACT.Copy).then_inc(s_gte, 1)

            def state_hi(i, c, j):
                wait(act, s_st, 28 * i + 7 * c + j)
                if j == 1:
                    wait(act, s_out, 16 * i + 4 * (c - 1))
                act.activation(state(st_sb[c % 2], 0, j), new_state(j), ACT.Copy).then_inc(s_sth, 1)

            def out_evac(i, c, v):
                o = 2 * (c % 2) + v // 2
                wait(act, s_out, 16 * i + 4 * c + v + 1)
                if v % 2 == 0:
                    wait(act, s_store[o], 64 * (2 * i + c // 2))
                act.activation(o_sb[o][:, 2 * (v % 2):2 * (v % 2) + 2, :].rearrange("p g t -> p (g t)"),
                               bank[:, 2 + v % 2, :], ACT.Copy, scale=1.0 / (US * KS)).then_inc(s_o1[v % 2], 1)

            evac_gt(0, 0)

            def slot(i, c):
                now, before, after = has(i, c), has(i, c - 1), has(i, c + 1)
                for what in ("s1", "s2", "s3", "o0", "s4", "s5", "o1", "s6", "s7", "o2", "g", "o3"):
                    k = int(what[1:] or 0)
                    if what[0] == "s" and now:
                        state_hi(i, c, k)
                    if what[0] == "o" and before:
                        out_evac(i, c - 1, k)
                    if what[0] == "g" and after:
                        evac_gt(i, c + 1)

            slots(act, slot)

        @block.vector
        def _(dve):
            do = Chain(dve, s_dve)

            def ts(o, a, s1, s2, op0, op1=None):
                do(dve.tensor_scalar(o, a, s1, s2, op0, op1) if op1 else dve.tensor_scalar(o, a, s1, None, op0))

            def tt(o, a, b, op):
                do(dve.tensor_tensor(out=o, in0=a, in1=b, op=op))

            def stt(o, a, s, b, op0, op1):
                do(dve.scalar_tensor_tensor(out=o, in0=a, scalar=s, in1=b, op0=op0, op1=op1))

            MUL, ADD, SUB = ALU.mult, ALU.add, ALU.subtract

            def exponential(o, v, k, r, p, ki):
                ts(r, v, 88.0, -87.0, ALU.min, ALU.max)
                ts(k, r, 1 / math.log(2.0), ROUND, MUL, ADD)
                ts(k, k, ROUND, None, SUB)
                stt(r, k, -LN2_HI, r, MUL, ADD)
                stt(r, k, -LN2_LO, r, MUL, ADD)
                ts(p, r, 1 / 5040, None, MUL)
                for d in (720, 120, 24, 6, 2, 1):
                    stt(p, p, 1 / d, r, ADD, MUL)
                ts(ki, k, 127.0, 2.0 ** 23, ADD, MUL)
                stt(o, p, 1.0, ki.bitcast(F32), ADD, MUL)

            dve.wait_ge(s_in[1], 16)
            dve.wait_ge(s_tr, 1)
            do(dve.tensor_copy(logs[:, 1, :], bank[:, 0, 0:P]))
            exponential(exps[:, :, :], logs[:, :, :], *(t[:, :, :] for t in ex), ex_i[:, :, :])
            dt, om, cy, f = exps[:, 0, :], omega[:, :], cycles[:, :], freq[:, :]
            do(dve.tensor_copy(ai[:, :], bank[:, 1, 0:P]))
            do(dve.tensor_copy(cr[:, :], bank[:, 2, 0:P]))
            do(dve.tensor_copy(ci[:, :], bank[:, 3, 0:P]))
            do(dve.tensor_copy(e_re[:, :], exps[:, 1, :]))
            tt(om, ai[:, :], dt, MUL)
            stt(dec[:, :], exps[:, 1, :], -1.0, dt, MUL, MUL)
            ts(cy, om, 1 / (2 * math.pi), ROUND, MUL, ADD)
            ts(cy, cy, ROUND, None, SUB)
            stt(om, cy, -TWO_PI_HI, om, MUL, ADD)
            stt(om, cy, -TWO_PI_LO, om, MUL, ADD)
            ts(f, om, 1 / (2 * math.pi), None, MUL)
            dve.wait_ge(s_p2, 1)
            tt(turns[:, :, :], ap(freq, 0, [[0, NS], [1, H]]), ap(p2, 0, [[1, NS], [0, H]]), MUL)
            ts(turns_r[:, :, :], turns[:, :, :], ROUND, ROUND, ADD, SUB)
            tt(turns[:, :, :], turns[:, :, :], turns_r[:, :, :], SUB)
            dve.sem_inc(s_turn, 1)
            dve.wait_ge(s_in[4], 16 * (NJ + 1))
            do(dve.tensor_copy(len_f[:, :], len_i[:, :]))
            ts(d_col[:, :], d_col[:, :], KS, KS, MUL, ADD)

            def split_x(G, half, quarter, r):
                dve.wait_ge(s_xh, unit(G, half, quarter, r) + 1)
                dve.tensor_tensor(out=x_lo[r % 2][:, :], in0=x_f[r][:, ::-1], in1=x_hi[r % 2][:, :],
                                  op=SUB).then_inc(s_xl, 1)

            def evac(G, half, quarter, r):
                for kk in range(2):
                    dve.wait_ge(s_uh, 2 * unit(G, half, quarter, r) + kk + 1)
                    at = 4 * kk * BG + 4 * quarter + r
                    dve.tensor_tensor(out=ap(u_stage[half], at + ROWS, [[BG, 4], [RUN, H]]),
                                      in0=bank[:, 2 * r + kk, :].rearrange("p (k d) -> p k d", k=4),
                                      in1=ap(u_stage[half], at, [[BG, 4], [RUN, H]]),
                                      op=SUB).then_inc(s_ul, 1)

            def group(G, half):
                for r in range(4):
                    split_x(G, half, 0, r)
                    if r:
                        evac(G, half, 0, r - 1)
                with dve.Fori(1, 4) as quarter:
                    for r in range(4):
                        split_x(G, half, quarter, r)
                        if r:
                            evac(G, half, quarter, r - 1)
                        else:
                            evac(G, half, quarter - 1, 3)
                evac(G, half, 3, 3)

            with dve.Fori(0, NG) as G:
                group(G, 0)
                group(G, 1)

            dve.wait_ge(s_kh, 1)
            do(dve.tensor_tensor(out=k_body[1][:, :, :].rearrange("p h a -> p (h a)"),
                                 in0=bank[0:16, 0:4, :].rearrange("p a b -> p (a b)"),
                                 in1=k_body[0][:, :, :].rearrange("p h a -> p (h a)"), op=SUB))
            do(dve.memset(k_head[:, :, :], 0.0))
            tt(k_zero[:, 0:1], bank[:, 4, 0:1], d_col[:, :], ADD)
            do(dve.tensor_copy(k_head[:, 0, P - 1:P], k_zero[:, 0:1]))
            tt(k_head[:, 1, P - 1:P], k_zero[:, 0:1], k_head[:, 0, P - 1:P], SUB)
            dve.sem_inc(s_kl, 1)
            dve.wait_ge(s_msk, 1)
            ts(row_i[:, :], row_i[:, :], NJ * Q - Q, None, ALU.bitwise_and)
            do(dve.tensor_copy(k_zero[:, 1:2], row_i[:, :]))
            for g in range(NG):
                tt(len_f[:, g:g + 1], len_f[:, g:g + 1], k_zero[:, 1:2], SUB)
                ts(mask[:, g, :], mask_i[:, :], len_f[:, g:g + 1], None, ALU.is_ge)
            dve.wait_ge(s_tab, 1)

            def make_g(i, c, step):
                r = c % 2
                if step == 0:
                    wait(dve, s_gx, 16 * i + 4 * c + 4)
                    dve.tensor_tensor(out=g_x[r][:, :, :], in0=g_x[r][:, :, :], in1=g_y[r][:, :, :], op=SUB)\
                        .then_inc(s_gw, 1)
                elif step == 1:
                    wait(dve, s_out, 16 * i + 4 * (c - 2))
                    dve.wait_ge(s_gw, 8 * i + 2 * c + 1)
                    dve.tensor_copy(g_sb[c % 4][:, :, 0, :], g_x[r][:, :, :]).then_inc(s_gw, 1)
                else:
                    dve.wait_ge(s_gw, 8 * i + 2 * c + 2)
                    dve.tensor_tensor(out=g_sb[c % 4][:, :, 1, :], in0=g_x[r][:, :, :],
                                      in1=g_sb[c % 4][:, :, 0, :], op=SUB).then_inc(s_g, 1)

            def make_lambda(i, c):
                wait(dve, s_st, 28 * i + 7 * (c - 1))
                for h in range(2):
                    col = bass.ds(8 * i + 2 * c + h, 1)
                    for k2 in range(2):
                        ins = dve.tensor_scalar(lam_t[:, 2 * h + k2, :], cross[:, :], lam[1][k2][:, col], None, MUL)
                ins.then_inc(s_lt, 1)
                dve.wait_ge(s_lt, 4 * i + c + 1)
                for h in range(2):
                    col = bass.ds(8 * i + 2 * c + h, 1)
                    for k2 in range(2):
                        ins = dve.scalar_tensor_tensor(out=lam_sb[c % 2][:, h, k2, :], in0=diag[:, :],
                                                       scalar=lam[0][k2][:, col], in1=lam_t[:, 2 * h + k2, :],
                                                       op0=MUL, op1=ADD)
                ins.then_inc(s_lam, 1)

            def state_lo(i, c, j):
                wait(dve, s_sth, 28 * i + 7 * c + j)
                dve.tensor_tensor(out=state(st_sb[c % 2], 1, j), in0=new_state(j),
                                  in1=state(st_sb[c % 2], 0, j), op=SUB).then_inc(s_stl, 1)

            def overlay(i, c, v):
                o = 2 * (c % 2) + v // 2
                wait(dve, s_o1[v % 2], 8 * i + 2 * c + v // 2 + 1)
                dve.memset(k_zero[0:1, 2 + v % 2:3 + v % 2], 0.0)
                g2 = slice(2 * (v % 2), 2 * (v % 2) + 2)
                dve.copy_predicated(o_sb[o][:, g2, :].rearrange("p g t -> p (g t)"),
                                    mask[:, g2, :].rearrange("p g t -> p (g t)"),
                                    bank[:, 4 + v % 2, :]).then_inc(s_o2[v % 2], 1)

            for step in range(3):
                make_g(0, 0, step)
            make_lambda(0, 0)

            def slot(i, c):
                now, before, after = has(i, c), has(i, c - 1), has(i, c + 1)
                for what in ("s1", "g0", "s2", "g1", "s3", "o0", "s4", "g2", "s5", "o1", "s6", "s7", "o2", "l", "o3"):
                    k2 = int(what[1:] or 0)
                    if what[0] == "s" and now:
                        state_lo(i, c, k2)
                    if what[0] == "o" and before:
                        overlay(i, c - 1, k2)
                    if what[0] == "g" and after:
                        make_g(i, c + 1, k2)
                    if what[0] == "l" and after:
                        make_lambda(i, c + 1)

            slots(dve, slot)


_INS = ["x", "itok_B_0_15", "itok_B_78_3631", "L0_cond_weights", "L1_cond_log_dt", "L1_cond_C",
        "L1_cond_log_A_real", "L1_cond_A_imag", "L1_cond_D"]


def kernel(**inputs):
    import numpy as _np
    import concourse.bacc as _bacc
    from concourse import mybir as _mybir
    from concourse.bass_utils import run_bass_kernel_spmd as _run

    nc = _bacc.Bacc("TRN2", target_bir_lowering=False, num_devices=1)
    arrays, args = {}, []
    for name in _INS:
        a = _np.ascontiguousarray(inputs[name])
        arrays[f"in_{name}"] = a
        args.append(nc.dram_tensor(f"in_{name}", a.shape, _mybir.dt.from_np(a.dtype), kind="ExternalInput").ap())
    shape = arrays["in_x"].shape
    args.append(nc.dram_tensor("out_0", shape, _mybir.dt.float32, kind="ExternalOutput").ap())
    build(nc, *args)
    r = _run(nc, [arrays], core_ids=[0])
    return r.results[0]["out_0"]
```

```python
import math
from contextlib import ExitStack

import concourse.bass as bass
from concourse import mybir

F32 = mybir.dt.float32
F16 = mybir.dt.float16
I32 = mybir.dt.int32
U8 = mybir.dt.uint8
ALU = mybir.AluOpType
ACT = mybir.ActivationFunctionType

P = 128
NB, H, T = 64, 128, 2048
NC = 16
NM = 64
KB = T // P
Q = 256
NJ = T // Q
BG = 16
NG = NB // BG
ROWS = NJ * BG
RUN = 2 * ROWS
EARLY, LATE = 4, 12
LATE_FAST = 8
HS = H // (EARLY + LATE)
HS_EARLY = H // 2 // EARLY
HT = H // 2
NS = 9
US = 8.0
KS = 256.0
ROUND = 1.5 * 2.0 ** 23
TWO_PI_HI = 6.28125
TWO_PI_LO = 2 * math.pi - TWO_PI_HI
LN2_HI = 0.693359375
LN2_LO = math.log(2.0) - LN2_HI
KROW = 3 * P


def ap(t, offset, dims, parts=P, first=0):
    width = 1
    for n in t.shape[1:]:
        width *= n
    return bass.AP(t, offset + first * width, [[width, parts]] + [list(d) for d in dims])


def build(nc, x, cond, length, w_in, log_dt, c_in, log_a, a_im, d_in, out):
    u_dram = nc.dram_tensor("u_scratch", [H, P, 2 * NG - 1, RUN], F16, kind="Internal")
    k_dram = nc.dram_tensor("k_scratch", [H, 2, KROW], F16, kind="Internal")

    ctx = ExitStack()
    with ctx:
        def sb(name, shape, dt, where=ctx):
            return where.enter_context(nc.sbuf_tensor(name, shape, dt))

        def sem(name):
            return ctx.enter_context(nc.semaphore(name))

        w_pair = sb("w_pair", [P, NC, 2, H], F16)
        cond_sb = sb("cond_sb", [1, NB], I32)
        len_i = sb("len_i", [P, NG], I32)
        len_f = sb("len_f", [P, NG], F32)
        row_i = sb("row_i", [P, 1], I32)
        d_col = sb("d_col", [P, 1], F32)
        flip = sb("flip", [P, P], F16)
        sign = sb("sign", [P, P], F16)
        diag = sb("diag", [P, P], F16)
        cross = sb("cross", [P, P], F16)
        scratch = ExitStack()
        waves = sb("waves", [P, 2 * NS + 1, H], F32, scratch)
        turns = waves[:, NS:2 * NS, :]
        wide = [sb(f"wide{i}", [P, NS, H], F32, scratch) for i in range(4)]
        ai, cr, ci, dec, e_re = (sb(n, [P, H], F32, scratch) for n in ("ai", "cr", "ci", "dec", "e_re"))
        p2 = sb("p2", [P, NS], F32, scratch)
        quarter_turn = sb("quarter_turn", [P, 1], F32, scratch)
        scratch.close()
        a_re, a_imt = (sb(f"alpha_{n}", [P, H, 16], F32) for n in ("re", "im"))
        b_re, b_imt = (sb(f"beta_{n}", [P, H, 16], F32) for n in ("re", "im"))
        s_re, s_im, k_b = (sb(n, [P, H], F32) for n in ("s_re", "s_im", "k_b"))
        used_up = ExitStack()
        c_top, k_a = (sb(n, [P, H], F32, used_up) for n in ("c_top", "k_a"))
        used_up.close()
        k_head = sb("k_head", [P, 2, P], F16)
        k_zero = sb("k_zero", [P, H], F32)
        lam_rh, lam_rl, lam_ih = (sb(f"lam_{n}", [P, H], F32) for n in ("rh", "rl", "ih"))
        tmp_t = sb("tmp_t", [P, 256], F32)
        powers = ExitStack()
        pw_re, pw_im = (sb(f"pw_{n}", [P, NS, H], F32, powers) for n in ("re", "im"))
        powers.close()
        factors = ExitStack()
        k_lhs = sb("k_lhs", [P, H, 16], F32, factors)
        factors.close()
        k_body = [sb(f"k_body{k}", [16, 2, HT, 16], F16) for k in range(2)]
        lam_il = sb("lam_il", [P, H], F32)
        sb("lam_pad", [P, H], F32)
        lam = [[lam_rh, lam_rl], [lam_ih, lam_il]]

        loop_x = ExitStack()
        x_f = [sb(f"x_f{i}", [P, T // 2], F32, loop_x) for i in range(4)]
        x_hi = [sb(f"x_hi{a}", [P, T // 2], F16, loop_x) for a in range(2)]
        x_lo = [sb(f"x_lo{a}", [P, T // 2], F16, loop_x) for a in range(2)]
        stage_0 = ExitStack()
        u_stage = [sb("u_stage0", [P, H, RUN], F16, stage_0)]
        start = ExitStack()
        ident = sb("ident", [P, P], F32, start)
        w_f = sb("w_f", [P, NC, H], F32, start)
        nat = [sb(f"nat{i}", [P, 2 * P], F32, start) for i in range(3)]
        logs = sb("logs", [P, 2, H], F32, start)
        exps = sb("exps", [P, 2, H], F32, start)
        turns_r = sb("turns_r", [P, NS, H], F32, start)
        ex = [sb(f"ex{i}", [P, 2, H], F32, start) for i in range(3)]
        ex_i = sb("ex_i", [P, 2, H], I32, start)
        omega, cycles, freq = (sb(n, [P, H], F32, start) for n in ("omega", "cycles", "freq"))
        start.close()
        stage_1 = ExitStack()
        u_stage += [sb("u_stage1", [P, H, RUN], F16, stage_1)]
        stage_1.close()
        stage_0.close()
        loop_x.close()
        B_BEFORE_STAGE_1 = sum(4 * T // 2 for _ in x_f) + 4 * (2 * T // 2) + 2 * H * RUN

        o_sb = [sb(f"o_sb{i}", [P, NG, Q], F32) for i in range(4)]
        st_sb = [sb(f"st_sb{i}", [P, 2, 2, NG, NJ, BG], F16) for i in range(2)]
        g_x = [sb(f"g_x{i}", [P, 2, Q], F32) for i in range(2)]
        g_y = [sb(f"g_y{i}", [P, 2, Q], F32) for i in range(2)]
        g_sb = [sb(f"g_sb{i}", [P, 2, 2, Q], F16) for i in range(4)]
        gt_sb = [sb(f"gt_sb{i}", [P, 2, 2, 2, P], F16) for i in range(2)]
        lam_sb = [sb(f"lam_sb{i}", [P, 2, 2, P], F16) for i in range(2)]
        lam_t = sb("lam_t", [P, 4, P], F16)
        mask_i = sb("mask_i", [P, Q], I32)
        mask = sb("mask", [P, NG, Q], U8)
        toep = [sb(f"toep{i}", [P, 2, 2, Q], F16) for i in range(2)]
        u_sb = [sb(f"u_sb{i}", [P, 2, 2, NG, 2, ROWS], F16) for i in range(4)]

        D_BYTES = (4 * 4 * NG * Q + 2 * 2 * 4 * NG * ROWS
                   + 4 * 4 * 2 * Q + 4 * 2 * 4 * Q
                   + 2 * 2 * 8 * P + 2 * 2 * 4 * P + 2 * 4 * P
                   + 4 * Q + NG * Q + 2 * 2 * 4 * Q
                   + 4 * 2 * 4 * NG * 2 * ROWS)
        assert D_BYTES <= B_BEFORE_STAGE_1

        bank = ctx.enter_context(nc.psum_tensor("bank", [P, 8, 512], F32))

        s_in = [sem(f"s_in{i}") for i in range(5)]
        s_const = sem("s_const")
        s_tr = sem("s_tr")
        s_dve = sem("s_dve")
        s_turn = sem("s_turn")
        s_wave = sem("s_wave")
        s_abs = sem("s_abs")
        s_p2 = sem("s_p2")
        s_wi, s_wh, s_wp = (sem(n) for n in ("s_wi", "s_wh", "s_wp"))
        s_x = [sem(f"s_x{i}") for i in range(4)]
        s_xh, s_xl, s_mm, s_uh, s_ul = (sem(n) for n in ("s_xh", "s_xl", "s_mm", "s_uh", "s_ul"))
        s_early = [sem(f"s_early{i}") for i in range(2)]
        s_late = [sem(f"s_late{i}") for i in range(2)]
        s_tab = sem("s_tab")
        s_msk = sem("s_msk")
        s_zero = sem("s_zero")
        s_km, s_kh, s_kl, s_kd = (sem(n) for n in ("s_km", "s_kh", "s_kl", "s_kd"))
        s_uc = sem("s_uc")
        s_u = [sem(f"s_u{i}") for i in range(4)]
        s_t = [sem(f"s_t{i}") for i in range(2)]
        s_gx, s_gw, s_g, s_lt, s_lam, s_gt, s_gte = (
            sem(n) for n in ("s_gx", "s_gw", "s_g", "s_lt", "s_lam", "s_gt", "s_gte"))
        s_st, s_sth, s_stl, s_out = (sem(n) for n in ("s_st", "s_sth", "s_stl", "s_out"))
        s_o1 = [sem(f"s_o1{i}") for i in range(2)]
        s_o2 = [sem(f"s_o2{i}") for i in range(2)]
        s_store = [sem(f"s_store{i}") for i in range(4)]

        N_BANKS = 4 * NB

        def stored(half, G):
            fast = 0 if half or (isinstance(G, int) and G == 0) else 2 if isinstance(G, int) and G == NG else 1
            return (s_early[half], 16 * EARLY * G), (s_late[half], 16 * (LATE * G - (LATE - LATE_FAST) * fast))

        block = ctx.enter_context(nc.Block())

        class Chain:
            def __init__(self, eng, s):
                self.eng, self.s, self.n = eng, s, 0

            def __call__(self, ins):
                ins.then_inc(self.s, 1)
                self.n += 1
                self.eng.wait_ge(self.s, self.n)

        def first_peeled(eng, body, after_first=None, shot=None):
            def group(G, half, start):
                with eng.Fori(start, 4) as quarter:
                    body(G, half, quarter)
            body(0, 0, 0)
            if after_first:
                after_first()
            group(0, 0, 1)
            group(0, 1, 0)
            with eng.Fori(1, NG - 1) as G:
                group(G, 0, 0)
                group(G, 1, 0)
            group(NG - 1, 0, 0)
            if shot:
                for quarter in range(2):
                    shot(quarter)
                    body(NG - 1, 1, quarter)
            group(NG - 1, 1, 2 if shot else 0)

        def unit(G, half, quarter, r):
            return 32 * G + 16 * half + 4 * quarter + r

        PAIRS = H // 2
        PEELED = 3
        LOOPS = (PAIRS - PEELED - 2) // 4

        def slots(eng, body):
            for s in range(PEELED):
                body(0, s)
            with eng.Fori(0, LOOPS) as i:
                for c in range(PEELED, PEELED + 4):
                    body(i, c)
            for s in range(4 * LOOPS + PEELED, PAIRS + 1):
                body(0, s)

        def has(i, c):
            return not isinstance(i, int) or 0 <= c < PAIRS

        def wait(eng, s, value):
            if not isinstance(value, int) or value > 0:
                eng.wait_ge(s, value)

        def state(t, part, j):
            return ap(t, part * NG * ROWS + j * BG, [[2 * NG * ROWS, 2], [ROWS, NG], [1, BG]])

        def new_state(j):
            return bank[:, 0:2, (j - 1) * NB:j * NB].rearrange("p h (g b) -> p h g b", b=BG)

        @block.sync
        def _(sp):
            sp.dma_start(nat[0][:, 0:NM], log_a[:, :]).then_inc(s_in[0], 16)
            sp.dma_start(nat[0][:, NM:P], log_a[:, :]).then_inc(s_in[0], 16)
            sp.dma_start(nat[1][:, 0:NM], a_im[:, :]).then_inc(s_in[0], 16)
            sp.dma_start(nat[1][:, NM:P], a_im[:, :]).then_inc(s_in[0], 16)
            sp.dma_start(nat[2][:, 0:P], c_in.rearrange("h n c -> h (n c)")).then_inc(s_in[0], 16)
            sp.dma_start(nat[2][:, P:2 * P], c_in.rearrange("h n c -> h (n c)")).then_inc(s_in[0], 16)
            sp.dma_start(cond_sb[:, :], cond.rearrange("(a b) -> a b", a=1)).then_inc(s_in[3], 16)
            def load_x(G, half, quarter):
                for r in range(4):
                    wait(sp, s_xl, unit(G, half, quarter, r) - 3)
                    blocks = x[16 * G + 4 * quarter + r, :, :].rearrange("c (j a t) -> c j a t", a=2, t=P)
                    sp.dma_start(x_f[r][:, :].rearrange("c (j t) -> c j t", t=P), blocks[:, :, half, :])\
                        .then_inc(s_x[r], 16)

            def load_rest():
                sp.dma_start(logs[:, 0, :], log_dt.partition_broadcast(P)).then_inc(s_in[1], 16)
                for j in range(NJ):
                    sp.dma_start(len_i[j * BG:(j + 1) * BG, :], length.rearrange("(g b) -> b g", b=BG),
                                 allow_slow_non_contiguous=True)\
                        .then_inc(s_in[4], 16)
                sp.dma_start(d_col[:, :], d_in.rearrange("(h a) -> h a", a=1)).then_inc(s_in[4], 16)

            first_peeled(sp, load_x, load_rest)

            for k in range(2):
                sp.wait_ge(s_kl, k + 1)
                for part in range(2):
                    dst = bass.AP(k_dram, (2 * HT * k + part) * KROW + P, [[16, 16], [2 * KROW, HT], [1, 16]])
                    sp.dma_start(dst, k_body[k][:, part, :, :]).then_inc(s_kd, 16)
            sp.dma_start(k_dram.ap()[:, :, 0:P], k_head[:, :, :]).then_inc(s_kd, 16)
            for s, value in (*stored(0, NG), *stored(1, NG - 1)):
                sp.wait_ge(s, value)

            def load_u(i, c):
                wait(sp, s_out, 16 * i + 4 * (c - 3))
                sp.dma_start(ap(u_sb[c % 4], 0, [[2 * NG * RUN, 2], [1, (2 * NG - 1) * RUN]]),
                             u_dram.ap()[bass.ds(8 * i + 2 * c, 2), :, :, :].rearrange("h p a r -> p h (a r)"))\
                    .then_inc(s_u[c % 4], 16)

            def load_toeplitz(i, c):
                src = bass.AP(k_dram, (8 * i + 2 * c) * (2 * KROW), [[1, P], [KROW, 4], [1, Q]])
                sp.dma_start(toep[c % 2][:, :, :, :].rearrange("p h a t -> p (h a) t"), src)\
                    .then_inc(s_t[c % 2], 16)

            load_u(0, 0)
            load_u(0, 1)
            sp.wait_ge(s_kd, 80)

            def slot(i, c):
                if has(i, c):
                    wait(sp, s_out, 16 * i + 4 * (c - 1))
                    load_toeplitz(i, c)
                if has(i, c + 2):
                    load_u(i, c + 2)
                if has(i, c - 1):
                    for h in range(2):
                        o = 2 * ((c - 1) % 2) + h
                        for g in range(NG):
                            if g % 2 == 0:
                                wait(sp, s_o2[g // 2], 8 * i + 2 * (c - 1) + h + 1)
                            dst = bass.AP(out.tensor, (8 * i + 2 * (c - 1) + h) * T + g * (BG * H * T),
                                          [[Q, NJ], [H * T, BG], [1, Q]])
                            sp.dma_start(dst, o_sb[o][:, g, :]).then_inc(s_store[o], 16)

            slots(sp, slot)
            for o in range(4):
                sp.wait_ge(s_store[o], 64 * (PAIRS // 2))

        @block.gpsimd
        def _(pool):
            do = Chain(pool, s_const)
            do(pool.memset(ident[:, :], 0.0))
            do(pool.affine_select(out=ident[:, :], in_=ident[:, :], compare_op=ALU.not_equal, fill=1.0,
                                  base=0, pattern=[[-1, P]], channel_multiplier=1))
            for n in range(NS):
                do(pool.memset(p2[:, n:n + 1], 2.0 ** n))
            do(pool.memset(quarter_turn[:, :], math.pi / 2))
            pool.sem_inc(s_p2, 1)
            for m in (flip, sign, diag, cross):
                do(pool.memset(m[:, :], 0.0))
            do(pool.affine_select(out=flip[:, :], in_=flip[:, :], compare_op=ALU.not_equal, fill=1.0 / US,
                                  base=-(P - 1), pattern=[[1, P]], channel_multiplier=1))
            do(pool.affine_select(out=diag[:, :], in_=diag[:, :], compare_op=ALU.not_equal, fill=1.0,
                                  base=0, pattern=[[-1, P]], channel_multiplier=1))
            for lo, col, m, fill in ((0, 0, sign, 1.0), (NM, NM, sign, -1.0),
                                     (0, NM, cross, 1.0), (NM, 0, cross, -1.0)):
                part = m[lo:lo + NM, col:col + NM]
                do(pool.affine_select(out=part, in_=part, compare_op=ALU.not_equal, fill=fill,
                                      base=0, pattern=[[-1, NM]], channel_multiplier=1))
            MUL, ADD, SUB = ALU.mult, ALU.add, ALU.subtract

            def ts(o, a, s1, s2, op0, op1=None):
                do(pool.tensor_scalar(o, a, s1, s2, op0, op1) if op1 else pool.tensor_scalar(o, a, s1, None, op0))

            def tt(o, a, b, op):
                do(pool.tensor_tensor(out=o, in0=a, in1=b, op=op))

            def rsqrt(y, d, t):
                ts(y.bitcast(I32), d.bitcast(I32), -0.5, float(0x5F3759DF), MUL, ADD)
                for _ in range(3):
                    tt(t, y, y, MUL)
                    tt(t, t, d, MUL)
                    ts(t, t, -0.5, 1.5, MUL, ADD)
                    tt(y, y, t, MUL)

            r, k, p, ki = (w[:, :, :] for w in wide)
            tw, amp = pw_im[:, :, :], pw_re[:, :, :]
            pool.wait_ge(s_turn, 1)
            tt(r, ap(dec, 0, [[0, NS], [1, H]]), ap(p2, 0, [[1, NS], [0, H]]), MUL)
            ts(r, r, 88.0, -87.0, ALU.min, ALU.max)
            ts(k, r, 1 / math.log(2.0), ROUND, MUL, ADD)
            ts(k, k, ROUND, None, SUB)
            for part in (LN2_HI, LN2_LO):
                ts(tw, k, -part, None, MUL)
                tt(r, r, tw, ADD)
            ts(p, r, 1 / 5040, None, MUL)
            for d in (720, 120, 24, 6, 2, 1):
                ts(p, p, 1 / d, None, ADD)
                tt(p, p, r, MUL)
            ts(ki.bitcast(I32), k, 127.0, 2.0 ** 23, ADD, MUL)
            ts(amp, p, 1.0, None, ADD)
            tt(amp, amp, ki, MUL)
            pool.wait_ge(s_wave, 1)
            tt(pw_im[:, :, :], amp, waves[:, 0:NS, :], MUL)
            tt(pw_re[:, :, :], amp, waves[:, NS:2 * NS, :], MUL)
            e2k, em1 = ki[:, 0, :], p[:, 0, :]
            tt(em1, em1, e2k, MUL)
            ts(e2k, e2k, -1.0, None, ADD)
            tt(em1, em1, e2k, ADD)
            l_re, l_im = pw_re[:, 0, :], pw_im[:, 0, :]
            (nr, qr, qi, tr, ti, t1, t2, t3, pr) = (wide[0][:, n, :] for n in range(NS))
            (pi, m2, yy, kk) = (wide[1][:, n, :] for n in range(4))
            cr_, ci_, ai_, er_ = cr[:, :], ci[:, :], ai[:, :], e_re[:, :]
            tt(nr, em1, waves[:, NS, :], MUL)
            tt(t1, waves[:, 2 * NS, :], waves[:, 2 * NS, :], MUL)
            ts(t1, t1, -2.0, None, MUL)
            tt(nr, nr, t1, ADD)

            def complex_mul(o_re, o_im, x_re, x_im, y_re, y_im):
                tt(t1, x_re, y_re, MUL)
                tt(t2, x_im, y_im, MUL)
                tt(o_re, t1, t2, SUB)
                tt(t1, x_re, y_im, MUL)
                tt(t2, x_im, y_re, MUL)
                tt(o_im, t1, t2, ADD)

            complex_mul(qr, qi, cr_, ci_, nr, l_im)
            tt(t1, er_, er_, MUL)
            tt(t2, ai_, ai_, MUL)
            tt(t1, t1, t2, ADD)
            ts(t3.bitcast(I32), t1.bitcast(I32), -1.0, float(0x7EF311C7), MUL, ADD)
            for _ in range(4):
                tt(t2, t1, t3, MUL)
                ts(t2, t2, -1.0, 2.0, MUL, ADD)
                tt(t3, t3, t2, MUL)
            ts(m2, er_, -1.0, None, MUL)
            ts(kk, ai_, -1.0, None, MUL)
            complex_mul(tr, ti, qr, qi, m2, kk)
            tt(tr, tr, t3, MUL)
            tt(ti, ti, t3, MUL)
            ts(tr, tr, 2 * KS, None, MUL)
            ts(ti, ti, 2 * KS, None, MUL)
            do(pool.tensor_copy(c_top[0:NM, :], tr[0:NM, :]))
            do(pool.memset(c_top[NM:P, :], 0.0))
            complex_mul(pr, pi, tr, ti, l_re, l_im)
            tt(t1, pr, pr, MUL)
            tt(t2, pi, pi, MUL)
            tt(m2, t1, t2, ADD)
            rsqrt(yy, m2, t1)
            tt(m2, m2, yy, MUL)
            ts(t3, pr, 0.0, None, ALU.is_ge)
            ts(t2, t3, 2.0, -1.0, MUL, ADD)
            tt(t2, t2, pr, MUL)
            tt(m2, m2, t2, ADD)
            ts(m2, m2, 0.5, None, MUL)
            rsqrt(yy, m2, t1)
            tt(t1, m2, yy, MUL)
            ts(qr, pi, 0.0, None, ALU.is_ge)
            ts(qr, qr, 2.0, -1.0, MUL, ADD)
            tt(t2, qr, pi, MUL)
            ts(t2, t2, 0.5, None, MUL)
            tt(t2, t2, yy, MUL)
            tt(kk, t1, t2, SUB)
            tt(kk, kk, t3, MUL)
            tt(s_re[:, :], t2, kk, ADD)
            tt(t1, t1, kk, SUB)
            tt(s_im[:, :], t1, qr, MUL)
            do(pool.tensor_copy(k_a[0:NM, :], s_re[0:NM, :]))
            do(pool.tensor_copy(k_a[NM:P, :], s_im[NM:P, :]))
            ts(k_b[0:NM, :], s_im[0:NM, :], -1.0, None, MUL)
            do(pool.tensor_copy(k_b[NM:P, :], s_re[NM:P, :]))
            for lo, sg in ((0, 1.0), (NM, -1.0)):
                rows = slice(lo, lo + NM)
                for t, s in ((a_re, s_re), (a_imt, s_im)):
                    do(pool.tensor_scalar(t[rows, :, 0:1].rearrange("p h a -> p (h a)"), s[rows, :], sg, None, ALU.mult))
            do(pool.memset(b_re[0:NM, :, 0:1], 1.0))
            do(pool.memset(b_imt[0:NM, :, 0:1], 0.0))
            do(pool.memset(b_re[NM:P, :, 0:1], 0.0))
            do(pool.memset(b_imt[NM:P, :, 0:1], -1.0))

            def product(dst, p1, f1, p2, f2, op, z0, z, hn):
                for h0 in range(0, H, hn):
                    v = lambda t, o: ap(t, h0 * 16 + o, [[16, hn], [1, z]])
                    f = lambda t, o: ap(t, o + h0, [[1, hn], [0, z]])
                    tmp = ap(tmp_t, 0, [[z, hn], [1, z]])
                    do(pool.tensor_tensor(out=v(dst, z0), in0=v(p1, 0), in1=f(*f1), op=ALU.mult))
                    do(pool.tensor_tensor(out=tmp, in0=v(p2, 0), in1=f(*f2), op=ALU.mult))
                    do(pool.tensor_tensor(out=v(dst, z0), in0=v(dst, z0), in1=tmp, op=op))

            for re, im, s0 in ((b_re, b_imt, 0), (a_re, a_imt, 4)):
                for lv in range(4):
                    z, fr, fi = 1 << lv, (pw_re, (s0 + lv) * H), (pw_im, (s0 + lv) * H)
                    hn = min(H, 256 // z)
                    product(re, re, fr, im, fi, ALU.subtract, z, z, hn)
                    product(im, re, fi, im, fr, ALU.add, z, z, hn)
            for (hi, lo), t in zip(lam, (pw_re, pw_im)):
                half = tmp_t[:, 0:NM].bitcast(F16)
                do(pool.tensor_copy(half, t[:, NS - 1, :]))
                do(pool.tensor_copy(hi[:, :], half))
                do(pool.tensor_tensor(out=lo[:, :], in0=t[:, NS - 1, :], in1=hi[:, :], op=ALU.subtract))
            product(k_lhs, a_re, (k_a, 0), a_imt, (k_b, 0), ALU.add, 0, 16, 16)
            pool.sem_inc(s_tab, 1)
            pool.wait_ge(s_early[0], 16 * EARLY * NG)
            do(pool.iota(mask_i[:, :], pattern=[[1, Q]], base=0, channel_multiplier=0))
            do(pool.iota(row_i[:, :], pattern=[[0, 1]], base=0, channel_multiplier=Q // BG))
            pool.sem_inc(s_msk, 1)

            def outer(i, c):
                r = c % 2
                wait(pool, s_g, 4 * i + c - 1)
                for dst, ta, tb in ((g_x, a_re, b_re), (g_y, a_imt, b_imt)):
                    for h in range(2):
                        o = (8 * i + 2 * c + h) * 16
                        pool.tensor_tensor(out=ap(dst[r], h * Q, [[16, 16], [1, 16]]),
                                           in0=ap(ta, o, [[1, 16], [0, 16]]),
                                           in1=ap(tb, o, [[0, 16], [1, 16]]), op=ALU.mult).then_inc(s_gx, 1)

            def copy_u(i, c):
                wait(pool, s_out, 16 * i + 4 * (c - 3))
                pool.tensor_copy(u_sb[c % 4][:, :, 1, NG - 1, :, :].rearrange("p h k r -> p h (k r)"),
                                 u_stage[1][:, bass.ds(8 * i + 2 * c, 2), :]).then_inc(s_uc, 1)

            outer(0, 0)
            pool.wait_ge(s_mm, N_BANKS + 2)
            pool.wait_ge(s_xl, 2 * NB)
            for t in st_sb:
                do(pool.memset(t[:, :, :, :, 0, :], 0.0))
            pool.sem_inc(s_zero, 1)
            pool.wait_ge(s_late[0], 16 * (LATE * NG - 2 * (LATE - LATE_FAST)))
            pool.wait_ge(s_ul, N_BANKS)
            copy_u(0, 0)
            copy_u(0, 1)

            def slot(i, c):
                if has(i, c + 1):
                    outer(i, c + 1)
                if has(i, c + 2):
                    copy_u(i, c + 2)

            slots(pool, slot)

        @block.tensor
        def _(pe):
            pe.wait_ge(s_const, 2)
            pe.wait_ge(s_in[0], 96)
            srcs = [nat[0][:, 0:P], nat[1][:, 0:P],
                    ap(nat[2], 0, [[P, 2], [2, NM]]), ap(nat[2], 1, [[P, 2], [2, NM]])]
            for k, src in enumerate(srcs):
                last = pe.transpose(bank[:, k, 0:P], src, ident[:, :])
            last.then_inc(s_tr, 1)
            pe.wait_ge(s_in[3], 16)
            pe.wait_ge(s_wp, 1)

            pe.sem_inc(s_mm, 2)

            def mix(G, half, quarter):
                after_taps = isinstance(quarter, int) and (G, half) == (NG - 1, 1)
                for r in range(4):
                    n = unit(G, half, quarter, r)
                    sel = pe.value_load(cond_sb[0:1, bass.ds(16 * G + 4 * quarter + r, 1)], min_val=0, max_val=NC - 1)
                    wait(pe, s_xh, n + 1)
                    wait(pe, s_xl, n + 1)
                    wait(pe, s_ul, 2 * n - 6)
                    if after_taps and r == 2:
                        pe.wait_ge(s_kl, quarter + 1)
                    for j in range(NJ):
                        back = slice((NJ - 1 - j) * P, (NJ - j) * P)
                        dst = bank[:, 2 * r + j // 4, (j % 4) * H:(j % 4 + 1) * H]
                        for m, (xs, part) in enumerate(((x_hi, 0), (x_hi, 1), (x_lo, 0))):
                            last = pe.matmul(dst, xs[r % 2][:, back],
                                             ap(w_pair, sel * (2 * H) + part * H, [[1, H]]),
                                             start=(m == 0), stop=(m == 2))
                        if j % 4 == 3:
                            last.then_inc(s_mm, 1)

            def taps(shot):
                pe.wait_ge(s_ul, 2 * unit(NG - 1, 1, shot, 0))
                pe.wait_ge(s_tab, 1)
                for h in range(HT):
                    last = pe.matmul(bank[0:16, 4 + h // 32, (h % 32) * 16:(h % 32 + 1) * 16],
                                     k_lhs[:, shot * HT + h, :], b_re[:, shot * HT + h, :], start=True, stop=True)
                if shot:
                    last = pe.matmul(bank[:, 6, 0:1], c_top[:, :], b_re[:, 0, 0:1], start=True, stop=True)
                last.then_inc(s_km, 1)

            first_peeled(pe, mix, shot=taps)

            def transpose_g(i, c):
                wait(pe, s_g, 4 * i + c + 1)
                wait(pe, s_gte, 8 * i + 2 * c)
                for h in range(2):
                    for tb in range(2):
                        for part in range(2):
                            last = pe.matmul(bank[:, 6 + h, (2 * tb + part) * P:(2 * tb + part + 1) * P],
                                             g_sb[c % 4][:, h, part, (1 - tb) * P:(2 - tb) * P], sign[:, :],
                                             start=True, stop=True)
                    last.then_inc(s_gt, 1)

            SPLIT = ((0, 0), (1, 0), (0, 1))

            def inputs_to_state(i, c):
                wait(pe, s_gte, 8 * i + 2 * c + 2)
                wait(pe, s_u[c % 4], 16 * (i + c // 4 + 1))
                wait(pe, s_uc, 4 * i + c + 1)
                wait(pe, s_stl, 28 * i + 7 * c)
                for h in range(2):
                    for m, (tb, (a, b)) in enumerate((tb, ab) for tb in range(2) for ab in SPLIT):
                        last = pe.matmul(bank[:, h, 0:(NJ - 1) * NB], gt_sb[c % 2][:, h, tb, a, :],
                                         ap(u_sb[c % 4], (2 * h + tb) * NG * RUN + b * ROWS,
                                            [[BG, NJ - 1], [RUN, NG], [1, BG]]),
                                         start=(m == 0), stop=(m == 5))
                last.then_inc(s_st, 1)

            def advance(i, c, j):
                wait(pe, s_lam, 4 * i + c + 1)
                wait(pe, s_sth, 28 * i + 7 * c + j)
                wait(pe, s_stl, 28 * i + 7 * c + j)
                for h in range(2):
                    for m, (a, b) in enumerate(SPLIT):
                        last = pe.matmul(bank[:, h, j * NB:(j + 1) * NB], lam_sb[c % 2][:, h, a, :],
                                         st_sb[c % 2][:, h, b, :, j, :], start=False, stop=(m == 2),
                                         skip_group_check=True)
                last.then_inc(s_st, 1)

            def out_part(i, c, n):
                h, gr = n // 4, n % 4
                u, g, t, st = u_sb[c % 4], g_sb[c % 4], toep[c % 2], st_sb[c % 2]
                y, ut = 2 + (n // 2) % 2, 4 + (n // 2) % 2
                col = (gr % 2) * Q
                if n == 0:
                    wait(pe, s_t[c % 2], 16 * (2 * i + c // 2 + 1))
                if n % 2 == 0:
                    wait(pe, s_o1[n // 2 % 2], 8 * i + 2 * c + n // 4)
                    wait(pe, s_o2[n // 2 % 2], 8 * i + 2 * c + n // 4)
                first = True
                for tb in range(2):
                    for a in range(2):
                        lhs = u[:, h, tb, gr, a, :]
                        for b in range(2 - a):
                            pe.matmul(bank[:, y, col + tb * P:col + Q], lhs, t[:, h, b, 0:Q - tb * P],
                                      start=first, stop=False, skip_group_check=True)
                            first = False
                        pe.matmul(bank[:, ut, col + tb * P:col + (tb + 1) * P], lhs, flip[:, :],
                                  start=(a == 0), stop=(a == 1), skip_group_check=True)
                for m, (a, b) in enumerate(SPLIT):
                    last = pe.matmul(bank[:, y, col:col + Q], st[:, h, a, gr, :, :].rearrange("p j b -> p (j b)"),
                                     g[:, h, b, :], start=False, stop=(m == 2), skip_group_check=True)
                if n % 2 == 1:
                    last.then_inc(s_out, 1)

            pe.wait_ge(s_ul, N_BANKS)
            transpose_g(0, 0)
            pe.wait_ge(s_zero, 1)

            def slot(i, c):
                now, before, after = has(i, c), has(i, c - 1), has(i, c + 1)
                if now:
                    inputs_to_state(i, c)
                for n in range(8):
                    if n == 6 and after:
                        transpose_g(i, c + 1)
                    if before:
                        if n == 0:
                            wait(pe, s_sth, 28 * i + 7 * c)
                            wait(pe, s_stl, 28 * i + 7 * c)
                        out_part(i, c - 1, n)
                    if now and n < NJ - 2:
                        advance(i, c, n + 1)

            slots(pe, slot)

        @block.scalar
        def _(act):
            act.dma_start(w_f[:, :, :], w_in.rearrange("s c d -> c s d")).then_inc(s_in[2], 16)
            act.wait_ge(s_wi, 1)
            act.activation(w_pair[:, :, 0, :], w_f[:, :, :], ACT.Copy, scale=US).then_inc(s_wh, 1)

            def waves_of_turns():
                act.wait_ge(s_turn, 1)
                act.wait_ge(s_p2, 1)
                act.activation(waves[:, 0:NS, :], turns, ACT.Sin, scale=6.283185)
                act.activation(waves[:, 2 * NS, :], waves[:, NS, :], ACT.Sin, scale=3.1415925).then_inc(s_abs, 1)
                act.wait_ge(s_abs, 1)
                act.activation(turns, turns, ACT.Abs).then_inc(s_abs, 1)
                act.wait_ge(s_abs, 2)
                act.activation(turns, turns, ACT.Sin, scale=-6.283185, bias=quarter_turn[:, 0:1])\
                    .then_inc(s_wave, 1)

            def split_x(G, half, quarter, r):
                n = unit(G, half, quarter, r)
                wait(act, s_x[r], 16 * (8 * G + 4 * half + quarter + 1))
                act.wait_ge(s_mm, 2 * n)
                act.activation(x_hi[r % 2][:, :], x_f[r][:, ::-1], ACT.Copy).then_inc(s_xh, 1)

            def evac(G, half, quarter, r):
                for k in range(2):
                    act.wait_ge(s_mm, 2 * unit(G, half, quarter, r) + k + 3)
                    act.activation(ap(u_stage[half], 4 * k * BG + 4 * quarter + r, [[BG, 4], [RUN, H]]),
                                   bank[:, 2 * r + k, :].rearrange("p (k d) -> p k d", k=4),
                                   ACT.Copy).then_inc(s_uh, 1)

            def store(G, half, first, count, s):
                hs = bass.ds(first, count)
                act.dma_start(u_dram.ap()[hs, :, NG * half + G, :].rearrange("h p r -> p h r"),
                              u_stage[half][:, hs, :]).then_inc(s, 16)

            def taps_hi(shot):
                act.wait_ge(s_km, shot + 1)
                act.activation(k_body[shot][:, 0, :, :].rearrange("p h a -> p (h a)"),
                               bank[0:16, 4:6, :].rearrange("p a b -> p (a b)"), ACT.Copy).then_inc(s_kh, 1)

            def group(G, half, before, first=False, shots=False):
                fast = first or shots
                for r in range(4):
                    split_x(G, half, 0, r)
                    if r == 1 and first:
                        waves_of_turns()
                    if r == 1 and shots:
                        taps_hi(0)
                    if r:
                        evac(G, half, 0, r - 1)
                    else:
                        for s, value in stored(half, G):
                            wait(act, s, value)
                    if before and (r == 0 or not first):
                        wait(act, s_ul, 2 * unit(*before, 4, 0))
                        for piece in range(EARLY) if first else (r,):
                            count = HS_EARLY if fast else HS
                            store(*before, count * piece, count, s_early[before[1]])

                def rest(quarter, storing):
                    for r in range(4):
                        split_x(G, half, quarter, r)
                        if r == 1 and shots and isinstance(quarter, int) and quarter == 1:
                            taps_hi(1)
                        if r:
                            evac(G, half, quarter, r - 1)
                        else:
                            evac(G, half, quarter - 1, 3)
                        if storing:
                            at = H // 2 - 4 * HS if fast else 0
                            store(*before, at + HS * (4 * quarter + r), HS, s_late[before[1]])

                if shots:
                    rest(1, True)
                    rest(2, True)
                    rest(3, False)
                elif first:
                    with act.Fori(1, 3) as quarter:
                        rest(quarter, True)
                    rest(3, False)
                else:
                    with act.Fori(1, 4) as quarter:
                        rest(quarter, before)
                evac(G, half, 3, 3)

            group(0, 0, None)
            group(0, 1, (0, 0), first=True)
            with act.Fori(1, NG - 1) as G:
                group(G, 0, (G - 1, 1))
                group(G, 1, (G, 0))
            group(NG - 1, 0, (NG - 2, 1))
            group(NG - 1, 1, (NG - 1, 0), shots=True)

            def evac_gt(i, c):
                for h in range(2):
                    wait(act, s_gt, 8 * i + 2 * c + h + 1)
                    wait(act, s_st, 28 * i + 7 * (c - 1) - 6)
                    act.activation(gt_sb[c % 2][:, h, :, :, :].rearrange("p a b m -> p (a b m)"),
                                   bank[:, 6 + h, :], ACT.Copy).then_inc(s_gte, 1)

            def state_hi(i, c, j):
                wait(act, s_st, 28 * i + 7 * c + j)
                if j == 1:
                    wait(act, s_out, 16 * i + 4 * (c - 1))
                act.activation(state(st_sb[c % 2], 0, j), new_state(j), ACT.Copy).then_inc(s_sth, 1)

            def out_evac(i, c, v):
                o = 2 * (c % 2) + v // 2
                wait(act, s_out, 16 * i + 4 * c + v + 1)
                if v % 2 == 0:
                    wait(act, s_store[o], 64 * (2 * i + c // 2))
                act.activation(o_sb[o][:, 2 * (v % 2):2 * (v % 2) + 2, :].rearrange("p g t -> p (g t)"),
                               bank[:, 2 + v % 2, :], ACT.Copy, scale=1.0 / (US * KS)).then_inc(s_o1[v % 2], 1)

            evac_gt(0, 0)

            def slot(i, c):
                now, before, after = has(i, c), has(i, c - 1), has(i, c + 1)
                for what in ("s1", "s2", "s3", "o0", "s4", "s5", "o1", "s6", "s7", "o2", "g", "o3"):
                    k = int(what[1:] or 0)
                    if what[0] == "s" and now:
                        state_hi(i, c, k)
                    if what[0] == "o" and before:
                        out_evac(i, c - 1, k)
                    if what[0] == "g" and after:
                        evac_gt(i, c + 1)

            slots(act, slot)

        @block.vector
        def _(dve):
            do = Chain(dve, s_dve)

            def ts(o, a, s1, s2, op0, op1=None):
                do(dve.tensor_scalar(o, a, s1, s2, op0, op1) if op1 else dve.tensor_scalar(o, a, s1, None, op0))

            def tt(o, a, b, op):
                do(dve.tensor_tensor(out=o, in0=a, in1=b, op=op))

            def stt(o, a, s, b, op0, op1):
                do(dve.scalar_tensor_tensor(out=o, in0=a, scalar=s, in1=b, op0=op0, op1=op1))

            MUL, ADD, SUB = ALU.mult, ALU.add, ALU.subtract

            def exponential(o, v, k, r, p, ki):
                ts(r, v, 88.0, -87.0, ALU.min, ALU.max)
                ts(k, r, 1 / math.log(2.0), ROUND, MUL, ADD)
                ts(k, k, ROUND, None, SUB)
                stt(r, k, -LN2_HI, r, MUL, ADD)
                stt(r, k, -LN2_LO, r, MUL, ADD)
                ts(p, r, 1 / 5040, None, MUL)
                for d in (720, 120, 24, 6, 2, 1):
                    stt(p, p, 1 / d, r, ADD, MUL)
                ts(ki, k, 127.0, 2.0 ** 23, ADD, MUL)
                stt(o, p, 1.0, ki.bitcast(F32), ADD, MUL)

            dve.wait_ge(s_in[2], 16)
            dve.wait_ge(s_const, 2)
            tt(w_f[:, :, :], w_f[:, :, :], ap(ident, 0, [[0, NC], [1, P]]), ADD)
            dve.sem_inc(s_wi, 1)
            dve.wait_ge(s_tr, 1)
            do(dve.tensor_copy(logs[:, 1, :], bank[:, 0, 0:P]))
            for k, t in enumerate((ai, cr, ci)):
                do(dve.tensor_copy(t[:, :], bank[:, k + 1, 0:P]))
            dve.wait_ge(s_wh, 1)
            stt(w_pair[:, :, 1, :], w_f[:, :, :], US, w_pair[:, :, 0, :], MUL, SUB)
            dve.sem_inc(s_wp, 1)

            def coefficients():
                dve.wait_ge(s_in[1], 16)
                exponential(exps[:, :, :], logs[:, :, :], *(t[:, :, :] for t in ex), ex_i[:, :, :])
                dt, om, cy, f = exps[:, 0, :], omega[:, :], cycles[:, :], freq[:, :]
                do(dve.tensor_copy(e_re[:, :], exps[:, 1, :]))
                tt(om, ai[:, :], dt, MUL)
                stt(dec[:, :], exps[:, 1, :], -1.0, dt, MUL, MUL)
                ts(cy, om, 1 / (2 * math.pi), ROUND, MUL, ADD)
                ts(cy, cy, ROUND, None, SUB)
                stt(om, cy, -TWO_PI_HI, om, MUL, ADD)
                stt(om, cy, -TWO_PI_LO, om, MUL, ADD)
                ts(f, om, 1 / (2 * math.pi), None, MUL)
                dve.wait_ge(s_p2, 1)
                tt(turns, ap(freq, 0, [[0, NS], [1, H]]), ap(p2, 0, [[1, NS], [0, H]]), MUL)
                ts(turns_r[:, :, :], turns, ROUND, ROUND, ADD, SUB)
                tt(turns, turns, turns_r[:, :, :], SUB)
                dve.sem_inc(s_turn, 1)
                dve.wait_ge(s_in[4], 16 * (NJ + 1))
                do(dve.tensor_copy(len_f[:, :], len_i[:, :]))
                ts(d_col[:, :], d_col[:, :], KS, KS, MUL, ADD)

            def split_x(G, half, quarter, r):
                dve.wait_ge(s_xh, unit(G, half, quarter, r) + 1)
                dve.tensor_tensor(out=x_lo[r % 2][:, :], in0=x_f[r][:, ::-1], in1=x_hi[r % 2][:, :],
                                  op=SUB).then_inc(s_xl, 1)

            def evac(G, half, quarter, r):
                for kk in range(2):
                    dve.wait_ge(s_uh, 2 * unit(G, half, quarter, r) + kk + 1)
                    at = 4 * kk * BG + 4 * quarter + r
                    dve.tensor_tensor(out=ap(u_stage[half], at + ROWS, [[BG, 4], [RUN, H]]),
                                      in0=bank[:, 2 * r + kk, :].rearrange("p (k d) -> p k d", k=4),
                                      in1=ap(u_stage[half], at, [[BG, 4], [RUN, H]]),
                                      op=SUB).then_inc(s_ul, 1)

            def taps_lo(shot):
                dve.wait_ge(s_kh, shot + 1)
                do(dve.tensor_tensor(out=k_body[shot][:, 1, :, :].rearrange("p h a -> p (h a)"),
                                     in0=bank[0:16, 4:6, :].rearrange("p a b -> p (a b)"),
                                     in1=k_body[shot][:, 0, :, :].rearrange("p h a -> p (h a)"), op=SUB))
                if shot:
                    do(dve.memset(k_head[:, :, :], 0.0))
                    tt(k_zero[:, 0:1], bank[:, 6, 0:1], d_col[:, :], ADD)
                    do(dve.tensor_copy(k_head[:, 0, P - 1:P], k_zero[:, 0:1]))
                    tt(k_head[:, 1, P - 1:P], k_zero[:, 0:1], k_head[:, 0, P - 1:P], SUB)
                dve.sem_inc(s_kl, 1)

            def group(G, half, shots=False):
                def four(quarter, shot=None):
                    for r in range(4):
                        split_x(G, half, quarter, r)
                        if r == 1 and shot is not None:
                            taps_lo(shot)
                        if r:
                            evac(G, half, quarter, r - 1)
                        elif not isinstance(quarter, int) or quarter:
                            evac(G, half, quarter - 1, 3)

                four(0, 0 if shots else None)
                if shots:
                    four(1, 1)
                with dve.Fori(1 + shots, 4) as quarter:
                    four(quarter)
                evac(G, half, 3, 3)

            group(0, 0)
            coefficients()
            group(0, 1)
            with dve.Fori(1, NG - 1) as G:
                group(G, 0)
                group(G, 1)
            group(NG - 1, 0)
            group(NG - 1, 1, shots=True)

            dve.wait_ge(s_tab, 1)

            def make_g(i, c, step):
                r = c % 2
                if step == 0:
                    wait(dve, s_gx, 16 * i + 4 * c + 4)
                    dve.tensor_tensor(out=g_x[r][:, :, :], in0=g_x[r][:, :, :], in1=g_y[r][:, :, :], op=SUB)\
                        .then_inc(s_gw, 1)
                elif step == 1:
                    wait(dve, s_out, 16 * i + 4 * (c - 2))
                    dve.wait_ge(s_gw, 8 * i + 2 * c + 1)
                    dve.tensor_copy(g_sb[c % 4][:, :, 0, :], g_x[r][:, :, :]).then_inc(s_gw, 1)
                else:
                    dve.wait_ge(s_gw, 8 * i + 2 * c + 2)
                    dve.tensor_tensor(out=g_sb[c % 4][:, :, 1, :], in0=g_x[r][:, :, :],
                                      in1=g_sb[c % 4][:, :, 0, :], op=SUB).then_inc(s_g, 1)

            def make_lambda(i, c):
                wait(dve, s_st, 28 * i + 7 * (c - 1))
                for h in range(2):
                    col = bass.ds(8 * i + 2 * c + h, 1)
                    for k2 in range(2):
                        ins = dve.tensor_scalar(lam_t[:, 2 * h + k2, :], cross[:, :], lam[1][k2][:, col], None, MUL)
                ins.then_inc(s_lt, 1)
                dve.wait_ge(s_lt, 4 * i + c + 1)
                for h in range(2):
                    col = bass.ds(8 * i + 2 * c + h, 1)
                    for k2 in range(2):
                        ins = dve.scalar_tensor_tensor(out=lam_sb[c % 2][:, h, k2, :], in0=diag[:, :],
                                                       scalar=lam[0][k2][:, col], in1=lam_t[:, 2 * h + k2, :],
                                                       op0=MUL, op1=ADD)
                ins.then_inc(s_lam, 1)

            def state_lo(i, c, j):
                wait(dve, s_sth, 28 * i + 7 * c + j)
                dve.tensor_tensor(out=state(st_sb[c % 2], 1, j), in0=new_state(j),
                                  in1=state(st_sb[c % 2], 0, j), op=SUB).then_inc(s_stl, 1)

            def overlay(i, c, v):
                o = 2 * (c % 2) + v // 2
                wait(dve, s_o1[v % 2], 8 * i + 2 * c + v // 2 + 1)
                dve.memset(k_zero[0:1, 2 + v % 2:3 + v % 2], 0.0)
                g2 = slice(2 * (v % 2), 2 * (v % 2) + 2)
                dve.copy_predicated(o_sb[o][:, g2, :].rearrange("p g t -> p (g t)"),
                                    mask[:, g2, :].rearrange("p g t -> p (g t)"),
                                    bank[:, 4 + v % 2, :]).then_inc(s_o2[v % 2], 1)

            for step in range(3):
                make_g(0, 0, step)
            make_lambda(0, 0)
            dve.wait_ge(s_msk, 1)
            ts(row_i[:, :], row_i[:, :], NJ * Q - Q, None, ALU.bitwise_and)
            do(dve.tensor_copy(k_zero[:, 1:2], row_i[:, :]))
            for g in range(NG):
                tt(len_f[:, g:g + 1], len_f[:, g:g + 1], k_zero[:, 1:2], SUB)
                ts(mask[:, g, :], mask_i[:, :], len_f[:, g:g + 1], None, ALU.is_ge)

            def slot(i, c):
                now, before, after = has(i, c), has(i, c - 1), has(i, c + 1)
                for what in ("s1", "g0", "s2", "g1", "s3", "o0", "s4", "g2", "s5", "o1", "s6", "s7", "o2", "l", "o3"):
                    k2 = int(what[1:] or 0)
                    if what[0] == "s" and now:
                        state_lo(i, c, k2)
                    if what[0] == "o" and before:
                        overlay(i, c - 1, k2)
                    if what[0] == "g" and after:
                        make_g(i, c + 1, k2)
                    if what[0] == "l" and after:
                        make_lambda(i, c + 1)

            slots(dve, slot)


_INS = ["x", "itok_B_0_15", "itok_B_78_3631", "L0_cond_weights", "L1_cond_log_dt", "L1_cond_C",
        "L1_cond_log_A_real", "L1_cond_A_imag", "L1_cond_D"]


def kernel(**inputs):
    import numpy as _np
    import concourse.bacc as _bacc
    from concourse import mybir as _mybir
    from concourse.bass_utils import run_bass_kernel_spmd as _run

    nc = _bacc.Bacc("TRN2", target_bir_lowering=False, num_devices=1)
    arrays, args = {}, []
    for name in _INS:
        a = _np.ascontiguousarray(inputs[name])
        arrays[f"in_{name}"] = a
        args.append(nc.dram_tensor(f"in_{name}", a.shape, _mybir.dt.from_np(a.dtype), kind="ExternalInput").ap())
    shape = arrays["in_x"].shape
    args.append(nc.dram_tensor("out_0", shape, _mybir.dt.float32, kind="ExternalOutput").ap())
    build(nc, *args)
    r = _run(nc, [arrays], core_ids=[0])
    return r.results[0]["out_0"]
```
